# Optimizing a Trainium2 kernel written in Bass

```python
import numpy as np
import jax
import jax.numpy as jnp

def _softmax(x, axis=-1):
    return jax.nn.softmax(x, axis=axis)

def _gelu(x):
    return jax.nn.gelu(x, approximate=True)

def _silu(x):
    return jax.nn.silu(x)

def _sigmoid(x):
    return jax.nn.sigmoid(x)

def _layernorm(x, axis=-1, eps=1e-05):
    m = jnp.mean(x, axis=axis, keepdims=True)
    v = jnp.var(x, axis=axis, keepdims=True)
    return (x - m) / jnp.sqrt(v + eps)

def _scatter_add(tgt, idx, src, axis=0):
    return tgt.at[idx].add(src)

def _segment_sum(src, seg, n):
    return jax.ops.segment_sum(src, seg, n)
kernel_name = 'mk_recurrent_d1_jaxref_r8_f6554f'

def setup_inputs(seed: int=0):
    np.random.seed(seed)
    _w = jnp.asarray

    def _L0_attn_setup():
        import jax, jax.numpy as jnp
        import numpy as np
        B, L, D = (2, 256, 256)
        H, G, E = (16, 4, 128)
        KV = H // G
        OUT = D
        key = jax.random.key(seed)
        ks = jax.random.split(key, 12)
        s_in = 1.0 / np.sqrt(D)
        s_o = 1.0 / np.sqrt(H * E)
        return {'x': jax.random.normal(ks[0], (B, L, D), jnp.float32), 'Wq': jax.random.normal(ks[1], (D, H * E), jnp.float32) * s_in, 'bq': jnp.zeros((H * E,), jnp.float32), 'Wk': jax.random.normal(ks[2], (D, KV * E), jnp.float32) * s_in, 'bk': jnp.zeros((KV * E,), jnp.float32), 'Wv': jax.random.normal(ks[3], (D, KV * E), jnp.float32) * s_in, 'bv': jnp.zeros((KV * E,), jnp.float32), 'Wo': jax.random.normal(ks[4], (H * E, OUT), jnp.float32) * s_o, 'bo': jnp.zeros((OUT,), jnp.float32), 'gamma': jnp.ones((OUT,), jnp.float32), 'beta': jnp.zeros((OUT,), jnp.float32)}
    _L0_attn_in = _L0_attn_setup()

    def _L0_ffn_setup():
        import jax, jax.numpy as jnp
        import numpy as np
        HIDDEN = 256
        INTER = 1024
        BATCH, LOCAL_SEQ = (2, 512)
        key = jax.random.key(seed)
        k1, k2, k3 = jax.random.split(key, 3)
        h_shard = jax.random.normal(k1, (BATCH, LOCAL_SEQ, HIDDEN), dtype=jnp.float32)
        w_gate_up = jax.random.normal(k2, (2 * INTER, HIDDEN), dtype=jnp.float32) * 0.02
        w_down = jax.random.normal(k3, (HIDDEN, INTER), dtype=jnp.float32) * 0.02
        return {'h_shard': h_shard, 'w_gate_up': w_gate_up, 'w_down': w_down}
    _L0_ffn_in = _L0_ffn_setup()
    _d = {'L0_attn_x': _L0_attn_in['x'], 'L0_attn_Wq': _L0_attn_in['Wq'], 'L0_attn_bq': _L0_attn_in['bq'], 'L0_attn_Wk': _L0_attn_in['Wk'], 'L0_attn_bk': _L0_attn_in['bk'], 'L0_attn_Wv': _L0_attn_in['Wv'], 'L0_attn_bv': _L0_attn_in['bv'], 'L0_attn_Wo': _L0_attn_in['Wo'], 'L0_attn_bo': _L0_attn_in['bo'], 'L0_attn_gamma': _L0_attn_in['gamma'], 'L0_attn_beta': _L0_attn_in['beta'], 'L0_ffn_w_gate_up': _L0_ffn_in['w_gate_up'], 'L0_ffn_w_down': _L0_ffn_in['w_down']}
    _x0 = _d['L0_attn_x']
    _d['L0_attn_x'] = jax.random.normal(jax.random.fold_in(jax.random.key(seed), 1), (4, 512, 256), dtype=_x0.dtype)
    del _x0
    return _d

def reference(L0_attn_x, L0_attn_Wq, L0_attn_bq, L0_attn_Wk, L0_attn_bk, L0_attn_Wv, L0_attn_bv, L0_attn_Wo, L0_attn_bo, L0_attn_gamma, L0_attn_beta, L0_ffn_w_gate_up, L0_ffn_w_down):

    def _L0_attn_ref(x, Wq, bq, Wk, bk, Wv, bv, Wo, bo, gamma, beta):
        import jax, jax.numpy as jnp
        import numpy as np
        B, L, D = (2, 256, 256)
        H, G, E = (16, 4, 128)
        KV = H // G
        OUT = D
        b, l, _ = x.shape
        Q = (x @ Wq + bq).reshape(b, l, H, E)
        K = (x @ Wk + bk).reshape(b, l, KV, E)
        V = (x @ Wv + bv).reshape(b, l, KV, E)
        K = jnp.broadcast_to(K[:, :, None, :, :], (b, l, G, KV, E)).reshape(b, l, H, E)
        V = jnp.broadcast_to(V[:, :, None, :, :], (b, l, G, KV, E)).reshape(b, l, H, E)
        scores = jnp.einsum('blhe,bmhe->bhlm', Q, K) / np.sqrt(E).astype(np.float32)
        mask = jnp.triu(jnp.ones((l, l), jnp.float32), k=1) * -1000000000.0
        attn = jax.nn.softmax(scores + mask[None, None, :, :], axis=-1)
        ctx = jnp.einsum('bhlm,bmhe->blhe', attn, V).reshape(b, l, H * E)
        y = jax.nn.gelu(ctx @ Wo + bo, approximate=False)
        r = x + y
        mu = jnp.mean(r, axis=-1, keepdims=True)
        var = jnp.var(r, axis=-1, keepdims=True)
        return (r - mu) * jax.lax.rsqrt(var + 1e-05) * gamma + beta

    def _L0_ffn_ref(h_shard, w_gate_up, w_down):
        import jax, jax.numpy as jnp
        import numpy as np
        HIDDEN = 256
        INTER = 1024
        BATCH, LOCAL_SEQ = (2, 512)
        batch, local_seq, hidden = h_shard.shape
        gate_up = jnp.einsum('bsh,oh->bso', h_shard, w_gate_up)
        gate, up = jnp.split(gate_up, 2, axis=-1)
        h = jax.nn.silu(gate) * up
        out = jnp.einsum('bsi,hi->bsh', h, w_down)
        return out
    x = L0_attn_x
    xn = _layernorm(x, axis=-1)
    s = _L0_attn_ref(xn, L0_attn_Wq, L0_attn_bq, L0_attn_Wk, L0_attn_bk, L0_attn_Wv, L0_attn_bv, L0_attn_Wo, L0_attn_bo, L0_attn_gamma, L0_attn_beta)
    g = _silu(_L0_ffn_ref(xn, L0_ffn_w_gate_up, L0_ffn_w_down))
    x = x + s * g
    return x

_drawn_inputs = setup_inputs


def setup_inputs(seed=0):
    import zlib

    import numpy as np

    out = dict(_drawn_inputs(seed))
    spreads = {'L0_attn_bq': (0.0, 0.8),
     'L0_attn_bk': (0.0, 0.8),
     'L0_attn_bv': (0.0, 0.8),
     'L0_attn_bo': (0.0, 0.8),
     'L0_attn_gamma': (1.0, 0.6),
     'L0_attn_beta': (0.0, 0.8)}
    factors = {'L0_attn_Wq': 8.0,
     'L0_attn_Wk': 8.0,
     'L0_attn_Wv': 8.0,
     'L0_attn_Wo': 8.0,
     'L0_ffn_w_gate_up': 2.798}
    for name, (base, spread) in spreads.items():
        noise = np.random.default_rng([zlib.crc32(name.encode()), seed]).standard_normal(out[name].shape)
        drawn = base * np.exp(spread * noise) if base else spread * noise
        out[name] = jnp.asarray(drawn.astype(out[name].dtype))
    for name, factor in factors.items():
        out[name] = (out[name] * factor).astype(out[name].dtype)
    return out
```

```python
import math
from contextlib import ExitStack

import numpy as np

import concourse.bass as bass
from concourse import mybir

F32 = mybir.dt.float32
F32R = mybir.dt.float32r
ALU = mybir.AluOpType
ACT = mybir.ActivationFunctionType

P = 128
B, L, D = 4, 512, 256
H, KV, E = 16, 4, 128
G = H // KV
F = 1024
DC = D // P
FC = F // P
T = L // P
EPS = 1e-5
SCALE = 1.0 / math.sqrt(E)
MASK = -1e9 / SCALE
BIG = 3.0e38
PASSES = ((0, 1), (1, 0), (0, 0))

PIECE = 2048
RAW_SLOTS = 2

UNITS = KV * T


def kv_of(u):
    return u // T


def tile_of(u):
    return T - 1 - u % T


def main_steps():
    for u in range(UNITS):
        n = tile_of(u) + 1
        for j in range(n):
            yield ("t", u, j)
            if j == 0 and u:
                yield ("o", u - 1)
            if j:
                yield ("p", u, j - 1)
        yield ("p", u, n - 1)
    yield ("o", UNITS - 1)


def side_steps():
    for kv in range(KV):
        yield from (("k", kv), ("v", kv))
        yield ("q", kv, 0)
        yield ("w", kv)
        yield from (("q", kv, g) for g in range(1, G))
        for i in range(T):
            yield from (("s", kv * T + i, g) for g in range(G))


def cost(step):
    kind = step[0]
    if kind in "kvq":
        return 3 * DC * L
    if kind == "w":
        return T * 2 * P
    if kind == "s":
        return 3 * max(2 * P, (tile_of(step[1]) + 1) * P)
    if kind == "t":
        return G * 2 * P
    if kind == "p":
        return 3 * G * P
    return 3 * G * D


LEAD = 5 * 3 * DC * L + T * 2 * P + 3 * DC * L + G * 3 * (L + (T - 1) * P)


def merged_steps():
    side = list(side_steps())
    main = list(main_steps())
    lead = LEAD
    side_all, main_all = sum(map(cost, side)), sum(map(cost, main[:main.index(("t", UNITS - 2, 0))]))
    out, done_side, done_main = [], 0, 0
    for m in main:
        while side and (done_side < lead + done_main * (side_all - lead) / main_all
                        or m[0] == "t" and ("s", m[1], G - 1) in side):
            out.append(side.pop(0))
            done_side += cost(out[-1])
        out.append(m)
        done_main += cost(m)
    return out


STEPS = merged_steps()
PROJ_OF_KV = 3 + G
PROJ_ALL = KV * PROJ_OF_KV
PROJ_INDEX = {s: n for n, s in enumerate(s for s in STEPS if s[0] in "kvwq")}
PAIR_INDEX = {s[1:]: n for n, s in enumerate(s for s in STEPS if s[0] == "t")}
PAIRS = len(PAIR_INDEX)
SCORES_ALL = UNITS * G
for _u in range(UNITS):
    assert STEPS.index(("s", _u, G - 1)) < STEPS.index(("t", _u, 0))
    assert _u < T or STEPS.index(("t", _u - T, tile_of(_u))) < STEPS.index(("s", _u, 0))


def build(nc, x, wq, wk, wv, wo, wgu, wd, bqkv, rows, ident_in, mask_in, g_scratch, out):
    ctx = ExitStack()

    def sb(name, shape, dt=F32, stack=ctx):
        return stack.enter_context(nc.sbuf_tensor(name, shape, dt))

    def pb(name, shape, stack=ctx):
        return stack.enter_context(nc.psum_tensor(name, shape, F32))

    def sem(name):
        return ctx.enter_context(nc.semaphore(name))

    def pair(name, shape, stack=ctx):
        return [sb(f"{name}_{part}", shape, F32R, stack) for part in ("hi", "lo")]

    def f32(ap):
        return ap.bitcast(F32)

    x_v = x.rearrange("b (t p) d -> b p t d", p=P)
    out_v = out.rearrange("b (t p) d -> b p t d", p=P)
    g_v = g_scratch.rearrange("b (t p) d -> b p t d", p=P)

    wq_s = pair("wq", [P, DC, H * E])
    wk_s = pair("wk", [P, DC, KV * E])
    wv_s = pair("wv", [P, DC, KV * E])
    wo_s = pair("wo", [P, H, D])
    xnT = pair("xnT", [P, DC, B * L])
    norm = sb("norm", [P, B, T, 2])
    bias = sb("bias", [P, H + 2 * KV])
    rowc = sb("rowc", [P, 3, D])
    ident = sb("ident", [P, P])
    mask = sb("mask", [P, L])
    neghalf = sb("neghalf", [P, T])
    bo_row, gamma_row, beta_row = (rowc[:, i, :] for i in range(3))

    early = ExitStack()
    wgu_s = pair("wgu", [P, DC, 2 * F], early)
    wd_s = pair("wd", [P, FC, D], early)
    raw = [sb(f"raw{i}", [P, PIECE], F32, early) for i in range(RAW_SLOTS)]
    first = ExitStack()
    x_all = sb("x_all", [P, B, T, D], F32, first)
    xn = sb("xn", [P, T, D], F32, first)
    stats1 = sb("stats1", [P, T, 6], F32, first)
    mv1 = sb("mv1", [P, T, 2], F32, first)
    ve1 = sb("ve1", [P, T], F32, first)
    first.close()
    gate = sb("gate", [P, 2, L], F32, early)
    hid = sb("hid", [P, 2, L], F32, early)
    hidT = [pair(f"hidT{i}", [P, L], early) for i in range(2)]
    g_out = sb("g_out", [P, T, D], F32, early)
    early.close()

    qT = [pair(f"qT{g}", [P, L]) for g in range(G)]
    kT = pair("kT", [P, L])
    vT = sb("vT", [P, L])
    v_s = [pair(f"v{i}", [P, T, E]) for i in range(2)]
    probs = [sb(f"probs{t}", [P, G, (t + 1) * P]) for t in range(T)]
    PT_SLOTS = 3
    pT = [pair(f"pT{i}", [P, G * P]) for i in range(PT_SLOTS)]
    cT = pair("cT", [P, G * P])
    y = sb("y", [P, T, D])
    least = sb("least", [P, UNITS, G])
    total = sb("total", [P, UNITS, G])
    inv = sb("inv", [P, UNITS, G])
    x_b = sb("x_b", [P, T, D])
    g_b = sb("g_b", [P, T, D])
    xn_b = sb("xn_b", [P, T, D])
    res = sb("res", [P, T, D])
    stats3 = sb("stats3", [P, T, 6])
    mv3 = sb("mv3", [P, T, 2])
    ve3 = sb("ve3", [P, T])
    rstd3 = sb("rstd3", [P, T])

    bank = [pb(f"bank{i}", [P, 4, P]) for i in range(4)]
    down_ps = pb("down_ps", [P, T, L])
    flat = [b[:].rearrange("p a n -> p (a n)") for b in bank]
    xT_ps = flat[0:2]
    gate_ps, up_ps = flat[0:2], flat[2:4]
    scores_ps = flat[0:2]
    probsT_ps = flat[2:4]
    proj_ps = [down_ps[:, 0, :], down_ps[:, 1, :]]
    ctx_ps = down_ps[:, 2, :]
    y_ps = down_ps[:, 3, 0:D]

    x_in, const_in = sem("x_in"), sem("const_in")
    raw_in = [sem(f"raw_in{i}") for i in range(RAW_SLOTS)]
    raw_hi, ffn_split, attn_split = sem("raw_hi"), sem("ffn_split"), sem("attn_split")
    stats_done, aggr_done, var_made, rstd_made = sem("stats_done"), sem("aggr_done"), sem("var_made"), sem("rstd_made")
    norm_kept, xn_made, xT_done, xT_hi, xT_split = sem("norm_kept"), sem("xn_made"), sem("xT_done"), sem("xT_hi"), sem("xT_split")
    gate_done, up_done, gate_silu, hid_made, hid_hi, hid_split = (
        sem("gate_done"), sem("up_done"), sem("gate_silu"), sem("hid_made"), sem("hid_hi"), sem("hid_split"))
    down_done, g_made, g_stored = sem("down_done"), sem("g_made"), sem("g_stored")
    proj_done, proj_hi, proj_split = sem("proj_done"), sem("proj_hi"), sem("proj_split")
    scores_done, masked, exp_done, inv_made, probs_made = (
        sem("scores_done"), sem("masked"), sem("exp_done"), sem("inv_made"), sem("probs_made"))
    probsT_done, probsT_hi, probsT_split = sem("probsT_done"), sem("probsT_hi"), sem("probsT_split")
    ctx_done, ctx_hi, ctx_split = sem("ctx_done"), sem("ctx_hi"), sem("ctx_split")
    y_done, y_added = sem("y_done"), sem("y_added")
    x_b_in, g_b_in, xn_b_made, gelu_done, res_made = (
        sem("x_b_in"), sem("g_b_in"), sem("xn_b_made"), sem("gelu_done"), sem("res_made"))
    stats3_done, aggr3_done, var3_made, rstd3_made, z_made, out_made, out_stored, pool_chain = (
        sem("stats3_done"), sem("aggr3_done"), sem("var3_made"), sem("rstd3_made"), sem("z_made"),
        sem("out_made"), sem("out_stored"), sem("pool_chain"))
    consts_set = sem("consts_set")

    wgu_v = wgu.rearrange("(c p) (g n) -> p c g n", p=P, g=2)
    wd_v = wd.rearrange("(c p) n -> p c n", p=P)
    wq_v = wq.rearrange("(c p) n -> p c n", p=P)
    wk_v = wk.rearrange("(c p) n -> p c n", p=P)
    wv_v = wv.rearrange("(c p) n -> p c n", p=P)
    wo_v = wo.rearrange("(h p) n -> p h n", p=P)
    half = F // 2
    pieces = []

    def gate_up_cols(w, lo, c):
        return w[:, c, :].rearrange("p (g n) -> p g n", g=2)[:, :, lo:lo + half]

    for lo in (0, half):
        pieces.append([(wgu_v[:, c, :, lo:lo + half], (c * 2 * half, 2 * half, 2),
                        [gate_up_cols(w, lo, c) for w in wgu_s]) for c in range(DC)])
    pieces.append([(wd_v, (0, FC * D, FC), [w[:, :, :] for w in wd_s])])
    pieces.append([(wk_v, (0, DC * KV * E, DC), [w[:, :, :] for w in wk_s]),
                   (wv_v, (DC * KV * E, DC * KV * E, DC), [w[:, :, :] for w in wv_s])])
    for c in range(DC):
        pieces.append([(wq_v[:, c:c + 1, :], (0, H * E, 1), [w[:, c:c + 1, :] for w in wq_s])])
    for i in range(2):
        hs = slice(i * H // 2, (i + 1) * H // 2)
        pieces.append([(wo_v[:, hs, :], (0, H // 2 * D, H // 2), [w[:, hs, :] for w in wo_s])])
    FFN_PIECES = 3
    FFN_PARTS = sum(len(p) for p in pieces[:FFN_PIECES])
    ALL_PARTS = sum(len(p) for p in pieces)

    def raw_view(k, at):
        start, width, n = at
        return raw[k % RAW_SLOTS][:, start:start + width].rearrange("p (a n) -> p a n", a=n)

    def parts():
        n = 0
        for k, piece in enumerate(pieces):
            for _, at, dst in piece:
                yield n, k, at, dst
                n += 1

    def landed(eng, k):
        eng.wait_ge(raw_in[k % RAW_SLOTS], 16 * len(pieces[k]) + 16 * sum(
            len(pieces[i]) for i in range(k % RAW_SLOTS, k, RAW_SLOTS)))

    block = ctx.enter_context(nc.Block())

    @block.sync
    def _(sp):
        for b in range(B):
            sp.dma_start(x_all[:, b], x_v[b]).then_inc(x_in, 16)
        sp.dma_start(ident[:], ident_in).then_inc(const_in, 16)
        done_parts = 0
        for k, piece in enumerate(pieces):
            if k >= RAW_SLOTS:
                done_parts += len(pieces[k - RAW_SLOTS])
                if k - RAW_SLOTS < FFN_PIECES:
                    sp.wait_ge(ffn_split, done_parts)
                else:
                    sp.wait_ge(attn_split, done_parts - FFN_PARTS)
            for src, at, _ in piece:
                sp.dma_start(raw_view(k, at), src).then_inc(raw_in[k % RAW_SLOTS], 16)
            if k == 0:
                sp.dma_start(mask[:], mask_in).then_inc(const_in, 16)
                sp.dma_start(bias[:], bqkv).then_inc(const_in, 16)
                sp.dma_start(rowc[:], rows).then_inc(const_in, 16)
        for b in range(B):
            sp.wait_ge(g_made, b + 1)
            sp.dma_start(g_v[b], g_out[:]).then_inc(g_stored, 16)
        sp.wait_ge(g_stored, 16 * B)
        sp.wait_ge(down_done, B)
        for b in range(B):
            sp.dma_start(x_b[:], x_v[b]).then_inc(x_b_in, 16)
            sp.dma_start(g_b[:], g_v[b]).then_inc(g_b_in, 16)
            sp.wait_ge(out_made, b + 1)
            sp.dma_start(out_v[b], res[:]).then_inc(out_stored, 16)
            sp.wait_ge(out_stored, 16 * b + 16)

    @block.gpsimd
    def _(pool):
        nc.gpsimd.memset(neghalf[:], -0.5).then_inc(pool_chain, 1)
        pool.wait_ge(pool_chain, 1)
        with pool.Fori(0, B) as b:
            pool.wait_ge(var_made, b + 1)
            nc.gpsimd.tensor_tensor(mv1[:, :, 1], ve1[:], neghalf[:], ALU.pow).then_inc(rstd_made, 1)
        for n, k, at, (hi, lo) in parts():
            if k >= FFN_PIECES:
                pool.wait_ge(raw_hi, n + 1)
                nc.gpsimd.tensor_tensor(lo, raw_view(k, at), f32(hi), ALU.subtract).then_inc(attn_split, 1)

        with pool.Fori(0, B) as b:
            chain = 0
            for step in STEPS:
                if step[0] == "s":
                    _, u, g = step
                    n = u * G + g
                    pool.wait_ge(inv_made, b * SCORES_ALL + n + 1)
                    p = probs[tile_of(u)][:, g, :]
                    nc.gpsimd.tensor_tensor(p, p, inv[:, u, g:g + 1].to_broadcast([P, (tile_of(u) + 1) * P]),
                                            ALU.mult).then_inc(probs_made, 1)
            pool.wait_ge(gelu_done, b + 1)
            pool.wait_ge(xn_b_made, b + 1)
            nc.gpsimd.tensor_tensor(res[:], res[:], xn_b[:], ALU.add).then_inc(res_made, 1)
            pool.wait_ge(var3_made, b + 1)
            nc.gpsimd.tensor_tensor(rstd3[:], ve3[:], neghalf[:], ALU.pow).then_inc(rstd3_made, 1)
            pool.wait_ge(z_made, b + 1)
            pool.wait_ge(g_b_in, 16 * b + 16)

            def over_tiles(row):
                return row.rearrange("p (a n) -> p a n", a=1).to_broadcast([P, T, D])

            for other, op in ((over_tiles(gamma_row), ALU.mult), (over_tiles(beta_row), ALU.add),
                              (g_b[:], ALU.mult)):
                nc.gpsimd.tensor_tensor(res[:], res[:], other, op).then_inc(pool_chain, 1)
                chain += 1
                pool.wait_ge(pool_chain, b * 3 + 1 + chain)
            nc.gpsimd.tensor_tensor(res[:], res[:], x_b[:], ALU.add).then_inc(out_made, 1)

    @block.scalar
    def _(act):
        def weight_hi(n, k, at, hi):
            landed(act, k)
            nc.scalar.activation(hi, raw_view(k, at), ACT.Copy).then_inc(raw_hi, 1)

        with act.Fori(0, B) as b:
            for c in range(DC):
                act.wait_ge(xT_done, b * DC + c + 1)
                nc.scalar.activation(xnT[0][:, c, bass.ds(b * L, L)], xT_ps[c], ACT.Copy).then_inc(xT_hi, 1)
        for n, k, at, (hi, lo) in parts():
            weight_hi(n, k, at, hi) if k < FFN_PIECES else None

        def chunk(b, c):
            act.wait_ge(gate_done, b * FC + c + 1)
            nc.scalar.activation(gate[:, c % 2], gate_ps[c % 2], ACT.Silu).then_inc(gate_silu, 1)
            act.wait_ge(hid_made, b * FC + c + 1)
            nc.scalar.activation(hidT[c % 2][0][:], hid[:, c % 2], ACT.Copy).then_inc(hid_hi, 1)

        for n, k, at, (hi, lo) in parts():
            weight_hi(n, k, at, hi) if k >= FFN_PIECES else None
        with act.Fori(0, B) as b:
            for c in range(FC):
                chunk(b, c)
            act.wait_ge(down_done, b + 1)
            nc.scalar.activation(g_out[:], down_ps[:, :, 0:D], ACT.Silu).then_inc(g_made, 1)
            act.wait_ge(g_stored, 16 * b + 16)

        with act.Fori(0, B) as b:
            for step in STEPS:
                if step[0] in "kwq":
                    n = PROJ_INDEX[step]
                    kv = step[1]
                    act.wait_ge(proj_done, b * PROJ_ALL + n + 1)
                    if step[0] == "k":
                        nc.scalar.activation(kT[0][:], proj_ps[n % 2], ACT.Identity,
                                             bias=bias[:, H + kv:H + kv + 1]).then_inc(proj_hi, 1)
                    elif step[0] == "q":
                        h = step[2] * KV + kv
                        nc.scalar.activation(qT[step[2]][0][:], proj_ps[n % 2], ACT.Identity,
                                             bias=bias[:, h:h + 1]).then_inc(proj_hi, 1)
                    else:
                        nc.scalar.activation(v_s[kv % 2][0][:].rearrange("p t e -> p (t e)"), proj_ps[n % 2],
                                             ACT.Copy).then_inc(proj_hi, 1)
                elif step[0] == "s":
                    _, u, g = step
                    n = u * G + g
                    p = probs[tile_of(u)][:, g, :]
                    act.wait_ge(masked, b * SCORES_ALL + n + 1)
                    nc.scalar.activation(p, p, ACT.Exp, bias=least[:, u, g:g + 1], scale=-1.0,
                                         accum_out=total[:, u, g:g + 1]).then_inc(exp_done, 1)
                elif step[0] == "t":
                    r = PAIR_INDEX[step[1:]]
                    act.wait_ge(probsT_done, b * PAIRS + r + 1)
                    nc.scalar.activation(pT[r % PT_SLOTS][0][:], probsT_ps[r % 2], ACT.Copy).then_inc(probsT_hi, 1)
                elif step[0] == "p" and step[2] == tile_of(step[1]):
                    act.wait_ge(ctx_done, b * UNITS + step[1] + 1)
                    nc.scalar.activation(cT[0][:], ctx_ps, ACT.Copy).then_inc(ctx_hi, 1)
            act.wait_ge(x_b_in, 16 * b + 16)
            act.wait_ge(y_added, b * UNITS + UNITS)
            nc.scalar.activation(res[:], y[:], ACT.Gelu).then_inc(gelu_done, 1)

    @block.vector
    def _(dve):
        dve.wait_ge(x_in, 16 * B)
        dve.wait_ge(const_in, 64)
        with dve.Fori(0, B) as b:
            for t in range(T):
                last = nc.vector.bn_stats(stats1[:, t, :], x_all[:, bass.ds(b, 1), t, :])
            last.then_inc(stats_done, 1)
            dve.wait_ge(stats_done, b + 1)
            nc.vector.memset(ve1[:], EPS)
            for t in range(T):
                last = nc.vector.bn_aggr(mv1[:, t, :], stats1[:, t, :])
            last.then_inc(aggr_done, 1)
            dve.wait_ge(aggr_done, b + 1)
            nc.vector.tensor_tensor(ve1[:], mv1[:, :, 1], ve1[:], ALU.add).then_inc(var_made, 1)
            dve.wait_ge(rstd_made, b + 1)
            nc.vector.tensor_copy(norm[:, bass.ds(b, 1)], mv1[:].rearrange("p (a t) k -> p a t k", a=1)).then_inc(norm_kept, 1)
            for t in range(T):
                last = nc.vector.tensor_scalar(xn[:, t, :], x_all[:, bass.ds(b, 1), t, :], mv1[:, t, 0:1],
                                               mv1[:, t, 1:2], ALU.subtract, ALU.mult)
            last.then_inc(xn_made, 1)
            for c in range(DC):
                dve.wait_ge(xT_hi, b * DC + c + 1)
                part = [w[:, c, bass.ds(b * L, L)] for w in xnT]
                nc.vector.tensor_tensor(part[1], xT_ps[c], f32(part[0]), ALU.subtract).then_inc(xT_split, 1)
        for n, k, at, (hi, lo) in parts():
            if k < FFN_PIECES:
                dve.wait_ge(raw_hi, n + 1)
                nc.vector.tensor_tensor(lo, raw_view(k, at), f32(hi), ALU.subtract).then_inc(ffn_split, 1)
        with dve.Fori(0, B) as b:
            for c in range(FC):
                dve.wait_ge(up_done, b * FC + c + 1)
                dve.wait_ge(gate_silu, b * FC + c + 1)
                nc.vector.tensor_tensor(hid[:, c % 2], gate[:, c % 2], up_ps[c % 2], ALU.mult).then_inc(hid_made, 1)
                dve.wait_ge(hid_hi, b * FC + c + 1)
                nc.vector.tensor_tensor(hidT[c % 2][1][:], hid[:, c % 2], f32(hidT[c % 2][0][:]),
                                        ALU.subtract).then_inc(hid_split, 1)

        def low_part(step, b):
            if step[0] == "t":
                r = PAIR_INDEX[step[1:]]
                dve.wait_ge(probsT_hi, b * PAIRS + r + 1)
                hi, lo = pT[r % PT_SLOTS]
                nc.vector.tensor_tensor(lo[:], probsT_ps[r % 2], f32(hi[:]), ALU.subtract).then_inc(probsT_split, 1)
            elif step[0] == "s":
                _, u, g = step
                dve.wait_ge(exp_done, b * SCORES_ALL + u * G + g + 1)
                nc.vector.reciprocal(inv[:, u, g:g + 1], total[:, u, g:g + 1]).then_inc(inv_made, 1)
            elif step[0] in "kwq":
                n = PROJ_INDEX[step]
                kv = step[1]
                dve.wait_ge(proj_hi, b * (PROJ_ALL - KV) + n + 1 - PROJ_V_BEFORE[n])
                if step[0] == "w":
                    hi, lo = (w[:].rearrange("p t e -> p (t e)") for w in v_s[kv % 2])
                    nc.vector.tensor_tensor(lo, proj_ps[n % 2], f32(hi), ALU.subtract).then_inc(proj_split, 1)
                else:
                    h = H + kv if step[0] == "k" else step[2] * KV + kv
                    hi, lo = kT if step[0] == "k" else qT[step[2]]
                    nc.vector.scalar_tensor_tensor(lo[:], proj_ps[n % 2], bias[:, h:h + 1], f32(hi[:]),
                                                   ALU.add, ALU.subtract).then_inc(proj_split, 1)
            else:
                dve.wait_ge(ctx_hi, b * UNITS + step[1] + 1)
                hi, lo = cT
                nc.vector.tensor_tensor(lo[:], ctx_ps, f32(hi[:]), ALU.subtract).then_inc(ctx_split, 1)

        with dve.Fori(0, B) as b:
            owed = None
            for step in STEPS:
                if step[0] == "s":
                    dve.wait_ge(scores_done, b * SCORES_ALL + step[1] * G + step[2] + 1)
                    if not owed:
                        nc.vector.memset(total[:, step[1], step[2]:step[2] + 1], 0.0)
                if owed:
                    low_part(owed, b)
                    owed = None
                if step[0] == "s":
                    _, u, g = step
                    t = tile_of(u)
                    n = u * G + g
                    nc.vector.tensor_tensor_reduce(
                        out=probs[t][:, g, :], in0=scores_ps[n % 2][:, 0:(t + 1) * P],
                        in1=mask[:, (T - 1 - t) * P:], scale=-SCALE, scalar=BIG, op0=ALU.add, op1=ALU.min,
                        accum_out=least[:, u, g:g + 1]).then_inc(masked, 1)
                    owed = step
                elif step[0] == "v":
                    n = PROJ_INDEX[step]
                    dve.wait_ge(proj_done, b * PROJ_ALL + n + 1)
                    h = H + KV + step[1]
                    nc.vector.tensor_scalar(vT[:], proj_ps[n % 2], bias[:, h:h + 1], None,
                                            ALU.add).then_inc(proj_split, 1)
                elif step[0] == "o":
                    u = step[1]
                    t = tile_of(u)
                    dve.wait_ge(y_done, b * UNITS + u + 1)
                    base = bo_row if kv_of(u) == 0 else y[:, t, :]
                    nc.vector.tensor_tensor(y[:, t, :], y_ps, base, ALU.add).then_inc(y_added, 1)
                elif step[0] == "p":
                    if step[2] == tile_of(step[1]):
                        owed = step
                else:
                    owed = step
            dve.wait_ge(x_b_in, 16 * b + 16)
            for t in range(T):
                last = nc.vector.tensor_scalar(xn_b[:, t, :], x_b[:, t, :], norm[:, bass.ds(b, 1), t, 0],
                                               norm[:, bass.ds(b, 1), t, 1], ALU.subtract, ALU.mult)
            last.then_inc(xn_b_made, 1)
            dve.wait_ge(res_made, b + 1)
            for t in range(T):
                last = nc.vector.bn_stats(stats3[:, t, :], res[:, t, :])
            last.then_inc(stats3_done, 1)
            dve.wait_ge(stats3_done, b + 1)
            nc.vector.memset(ve3[:], EPS)
            for t in range(T):
                last = nc.vector.bn_aggr(mv3[:, t, :], stats3[:, t, :])
            last.then_inc(aggr3_done, 1)
            dve.wait_ge(aggr3_done, b + 1)
            nc.vector.tensor_tensor(ve3[:], mv3[:, :, 1], ve3[:], ALU.add).then_inc(var3_made, 1)
            dve.wait_ge(rstd3_made, b + 1)
            for t in range(T):
                last = nc.vector.tensor_scalar(res[:, t, :], res[:, t, :], mv3[:, t, 0:1], rstd3[:, t:t + 1],
                                               ALU.subtract, ALU.mult)
            last.then_inc(z_made, 1)

    @block.tensor
    def _(pe):
        def product(dst, left, right, first, last):
            for i, (a, c) in enumerate(PASSES):
                ins = nc.tensor.matmul(dst, left[a], right[c], start=first and i == 0,
                                       stop=last and i == len(PASSES) - 1)
            return ins

        pe.wait_ge(const_in, 64)
        with pe.Fori(0, B) as b:
            pe.wait_ge(xn_made, b + 1)
            for c in range(DC):
                for t in range(T):
                    last = nc.tensor.transpose(xT_ps[c][:, t * P:(t + 1) * P], xn[:, t, c * P:(c + 1) * P], ident[:])
                last.then_inc(xT_done, 1)
            pe.wait_ge(xT_split, b * DC + DC)

        def gate_up(b, c):
            if c >= 2:
                pe.wait_ge(hid_made, b * FC + c - 1)
            for i, (ps, done) in enumerate(((gate_ps, gate_done), (up_ps, up_done))):
                at = i * F + c * P
                for k in range(DC):
                    last = product(ps[c % 2], [w[:, k, at:at + P] for w in wgu_s],
                                   [w[:, k, bass.ds(b * L, L)] for w in xnT], k == 0, k == DC - 1)
                last.then_inc(done, 1)

        def down(b, c):
            pe.wait_ge(hid_split, b * FC + c + 1)
            for t in range(T):
                last = product(down_ps[:, t, 0:D], [w[:, t * P:(t + 1) * P] for w in hidT[c % 2]],
                               [w[:, c, :] for w in wd_s], c == 0, c == FC - 1)
            return last

        pe.wait_ge(ffn_split, FFN_PARTS)
        with pe.Fori(0, B) as b:
            for c in range(FC):
                gate_up(b, c)
                if c:
                    down(b, c - 1)
            down(b, FC - 1).then_inc(down_done, 1)

        def project(b, step):
            kind, kv = step[0], step[1]
            n = PROJ_INDEX[step]
            if n >= 2:
                pe.wait_ge(proj_split, b * PROJ_ALL + n - 1)
            if kind == "w":
                pe.wait_ge(proj_split, b * PROJ_ALL + PROJ_INDEX[("v", kv)] + 1)
                for j in range(T):
                    last = nc.tensor.transpose(proj_ps[n % 2][:, j * P:(j + 1) * P], vT[:, j * P:(j + 1) * P], ident[:])
            else:
                w_s = {"k": wk_s, "v": wv_s, "q": wq_s}[kind]
                at = (step[2] * KV + kv if kind == "q" else kv) * E
                for c in range(DC):
                    last = product(proj_ps[n % 2], [w[:, c, at:at + E] for w in w_s],
                                   [w[:, c, bass.ds(b * L, L)] for w in xnT], c == 0, c == DC - 1)
            last.then_inc(proj_done, 1)

        def scores(b, u, g):
            n = u * G + g
            t = tile_of(u)
            pe.wait_ge(proj_split, b * PROJ_ALL + PROJ_INDEX[("q", kv_of(u), g)] + 1)
            if n >= 2:
                pe.wait_ge(masked, b * SCORES_ALL + n - 1)
            width = max(2, t + 1) * P
            product(scores_ps[n % 2][:, 0:width], [w[:, t * P:(t + 1) * P] for w in qT[g]],
                    [w[:, 0:width] for w in kT], True, True).then_inc(scores_done, 1)

        def transposes(b, u, j):
            r = PAIR_INDEX[(u, j)]
            if j == 0:
                pe.wait_ge(probs_made, b * SCORES_ALL + (u + 1) * G)
            if r >= 2:
                pe.wait_ge(probsT_split, b * PAIRS + r - 1)
            for g in range(G):
                last = nc.tensor.transpose(probsT_ps[r % 2][:, g * P:(g + 1) * P],
                                           probs[tile_of(u)][:, g, j * P:(j + 1) * P], ident[:])
            last.then_inc(probsT_done, 1)

        def values(b, u, j):
            r = PAIR_INDEX[(u, j)]
            pe.wait_ge(probsT_split, b * PAIRS + r + 1)
            if j == 0:
                pe.wait_ge(proj_split, b * PROJ_ALL + PROJ_INDEX[("w", kv_of(u))] + 1)
                if u:
                    pe.wait_ge(ctx_split, b * UNITS + u)
            last = product(ctx_ps, [w[:, j, :] for w in v_s[kv_of(u) % 2]], [w[:] for w in pT[r % PT_SLOTS]],
                           j == 0, j == tile_of(u))
            if j == tile_of(u):
                last.then_inc(ctx_done, 1)

        def output(b, u):
            pe.wait_ge(ctx_split, b * UNITS + u + 1)
            if u:
                pe.wait_ge(y_added, b * UNITS + u)
            for g in range(G):
                last = product(y_ps, [w[:, g * P:(g + 1) * P] for w in cT], [w[:, g * KV + kv_of(u), :] for w in wo_s],
                               g == 0, g == G - 1)
            last.then_inc(y_done, 1)

        pe.wait_ge(attn_split, ALL_PARTS - FFN_PARTS)
        pe.wait_ge(g_made, B)
        with pe.Fori(0, B) as b:
            for step in STEPS:
                if step[0] in "kvwq":
                    project(b, step)
                elif step[0] == "s":
                    scores(b, *step[1:])
                elif step[0] == "t":
                    transposes(b, *step[1:])
                elif step[0] == "p":
                    values(b, *step[1:])
                else:
                    output(b, step[1])

    ctx.close()


PROJ_V_BEFORE = [sum(s[0] == "v" and PROJ_INDEX[s] < n for s in PROJ_INDEX) for n in range(PROJ_ALL)]


def kernel(**inputs):
    import concourse.bacc as bacc
    from concourse.bass_utils import run_bass_kernel_spmd

    def get(name):
        return np.asarray(inputs["L0_" + name])

    def by_head(a):
        return a.reshape(-1, E).T

    keys = np.arange(P)
    mask = np.zeros((P, L), np.float32)
    mask[:, L - P:] = np.where(keys[None, :] > keys[:, None], np.float32(MASK), np.float32(0))
    arrays = {
        "x": get("attn_x"),
        "wq": get("attn_Wq"),
        "wk": get("attn_Wk"),
        "wv": get("attn_Wv"),
        "wo": get("attn_Wo"),
        "wgu": get("ffn_w_gate_up").T,
        "wd": get("ffn_w_down").T,
        "bqkv": np.concatenate([by_head(get("attn_bq")), by_head(get("attn_bk")), by_head(get("attn_bv"))], axis=1),
        "rows": np.broadcast_to(np.stack([get("attn_bo"), get("attn_gamma"), get("attn_beta")]), (P, 3, D)),
        "ident": np.eye(P, dtype=np.float32),
        "mask": mask,
    }
    arrays = {f"in_{k}": np.ascontiguousarray(v) for k, v in arrays.items()}
    nc = bacc.Bacc("TRN2", target_bir_lowering=False, num_devices=1)
    args = [nc.dram_tensor(k, a.shape, F32, kind="ExternalInput").ap() for k, a in arrays.items()]
    g_scratch = nc.dram_tensor("g_scratch", (B, L, D), F32, kind="Internal").ap()
    out = nc.dram_tensor("out", (B, L, D), F32, kind="ExternalOutput").ap()
    build(nc, *args, g_scratch, out)
    r = run_bass_kernel_spmd(nc, [arrays], core_ids=[0])
    return r.results[0]["out"]
```

```python
import math
from contextlib import ExitStack

import numpy as np

import concourse.bass as bass
from concourse import mybir

F32 = mybir.dt.float32
F32R = mybir.dt.float32r
ALU = mybir.AluOpType
ACT = mybir.ActivationFunctionType

P = 128
B, L, D = 4, 512, 256
H, KV, E = 16, 4, 128
G = H // KV
F = 1024
DC = D // P
FC = F // P
T = L // P
EPS = 1e-5
SCALE = 1.0 / math.sqrt(E)
MASK = -1e9 / SCALE
BIG = 3.0e38
PASSES = ((0, 1), (1, 0), (0, 0))

PIECE = 2048
INVERSE_LAG = 2
RAW_SLOTS = 2

SEGMENT = """
t3.0 s1.0 o t3.1 s1.1 p3.0 s1.2 t3.2 s1.3 p3.1 s0.0 s0.1 t3.3 s0.2 p3.2 s0.3 K p3.3
t2.0 V o t2.1 Q0 p2.0 W t2.2 Q1 p2.1 Q2 p2.2
t1.0 Q3 o S3.0 t1.1 p1.0 S3.1 p1.1 S3.2
t0.0 S3.3 o S2.0 S2.1 p0.0 S2.2 S2.3
"""
AHEAD = "K V Q0 W Q1 Q2 Q3 S3.0 S3.1 S3.2 S3.3 S2.0 S2.1 S2.2 S2.3"
UNITS = KV * T
PROJ_OF_KV = 3 + G
PROJ_ALL = KV * PROJ_OF_KV
PAIRS_OF_KV = T * (T + 1) // 2
PAIRS = KV * PAIRS_OF_KV
SCORES_ALL = UNITS * G


def kv_of(u):
    return u // T


def tile_of(u):
    return T - 1 - u % T


def segment(kv, last=False, text=SEGMENT):
    unit = None
    for word in text.split():
        kind, rest = word[0], word[1:]
        if kind in "KVWQS" and last:
            continue
        of = kv + 1 if kind in "KVWQS" else kv
        kind = kind.lower()
        if kind == "q":
            yield kind, of, int(rest)
        elif kind in "kvw":
            yield kind, of
        elif kind == "o":
            if unit:
                yield kind, unit - 1
        else:
            t, i = map(int, rest.split("."))
            u = of * T + T - 1 - t
            if kind == "t":
                unit = u
            yield kind, u, i
    if last:
        yield "o", unit


def proj_index(step):
    return step[1] * PROJ_OF_KV + ["k", "v", "q0", "w", "q1", "q2", "q3"].index(step[0] + "".join(map(str, step[2:])))


def pair_index(u, j):
    return kv_of(u) * PAIRS_OF_KV + sum(tile + 1 for tile in range(tile_of(u) + 1, T)) + j


def vector_steps(steps):
    steps = list(steps)
    order = []
    for i, step in enumerate(steps):
        before = [x for x in steps[max(0, i - INVERSE_LAG):i + 1] if x[0] == "s"]
        if step[0] == "s":
            order.append(("masked", *step[1:]))
        takes_low = [x for x in steps[max(0, i - 1):i] if x[0] in "kwqt" or x[0] == "p" and x[2] == tile_of(x[1])]
        order += [("low", x) for x in takes_low]
        if i >= INVERSE_LAG and steps[i - INVERSE_LAG][0] == "s":
            order.append(("inv", *steps[i - INVERSE_LAG][1:]))
        if step[0] in "vo":
            order.append(step)
        assert step[0] != "t" or ("s", step[1], G - 1) not in before
    tail = steps[-INVERSE_LAG:]
    if tail[-1][0] in "kwqt" or tail[-1][0] == "p":
        order.append(("low", tail[-1]))
    order += [("inv", *x[1:]) for x in tail if x[0] == "s"]
    return order


def build(nc, x, wq, wk, wv, wo, wgu, wd, bqkv, rows, ident_in, mask_in, g_scratch, out):
    ctx = ExitStack()

    def sb(name, shape, dt=F32, stack=ctx):
        return stack.enter_context(nc.sbuf_tensor(name, shape, dt))

    def pb(name, shape, stack=ctx):
        return stack.enter_context(nc.psum_tensor(name, shape, F32))

    def sem(name):
        return ctx.enter_context(nc.semaphore(name))

    def pair(name, shape, stack=ctx):
        return [sb(f"{name}_{part}", shape, F32R, stack) for part in ("hi", "lo")]

    def f32(ap):
        return ap.bitcast(F32)

    x_v = x.rearrange("b (t p) d -> b p t d", p=P)
    out_v = out.rearrange("b (t p) d -> b p t d", p=P)
    g_v = g_scratch.rearrange("b (t p) d -> b p t d", p=P)

    wq_s = pair("wq", [P, DC, H * E])
    wk_s = pair("wk", [P, DC, KV * E])
    wv_s = pair("wv", [P, DC, KV * E])
    wo_s = pair("wo", [P, H, D])
    xnT = pair("xnT", [P, DC, B * L])
    norm = sb("norm", [P, B * T, 2])
    bias = sb("bias", [P, H + 2 * KV])
    rowc = sb("rowc", [P, 3, D])
    ident = sb("ident", [P, P])
    mask = sb("mask", [P, L])
    neghalf = sb("neghalf", [P, B * T])
    bo_row, gamma_row, beta_row = (rowc[:, i, :] for i in range(3))

    early = ExitStack()
    wgu_s = pair("wgu", [P, DC, 2 * F], early)
    wd_s = pair("wd", [P, FC, D], early)
    raw = [sb(f"raw{i}", [P, PIECE], F32, early) for i in range(RAW_SLOTS)]
    first = ExitStack()
    x_all = sb("x_all", [P, B, T, D], F32, first)
    xn = sb("xn", [P, 2, T, D], F32, first)
    stats1 = sb("stats1", [P, B * T, 6], F32, first)
    ve1 = sb("ve1", [P, B * T], F32, first)
    first.close()
    gate = sb("gate", [P, 2, L], F32, early)
    hid = sb("hid", [P, 2, L], F32, early)
    hidT = [pair(f"hidT{i}", [P, L], early) for i in range(2)]
    g_out = sb("g_out", [P, T, D], F32, early)
    early.close()

    qT = [pair(f"qT{g}", [P, L]) for g in range(G)]
    kT = pair("kT", [P, L])
    vT = sb("vT", [P, L])
    v_s = [pair(f"v{i}", [P, T, E]) for i in range(2)]
    probs = [sb(f"probs{t}", [P, G, (t + 1) * P]) for t in range(T)]
    pT = [pair(f"pT{i}", [P, G * P]) for i in range(2)]
    cT = pair("cT", [P, G * P])
    y = sb("y", [P, T, D])
    least = sb("least", [P, UNITS, G])
    total = sb("total", [P, UNITS, G])
    inv = sb("inv", [P, UNITS, G])
    x_b = sb("x_b", [P, T, D])
    g_b = sb("g_b", [P, T, D])
    xn_b = sb("xn_b", [P, T, D])
    res = sb("res", [P, T, D])
    stats3 = sb("stats3", [P, T, 6])
    mv3 = sb("mv3", [P, T, 2])
    ve3 = sb("ve3", [P, T])
    rstd3 = sb("rstd3", [P, T])

    bank = [pb(f"bank{i}", [P, 4, P]) for i in range(4)]
    down_ps = pb("down_ps", [P, T, L])
    flat = [b[:].rearrange("p a n -> p (a n)") for b in bank]
    xT_ps = [flat[0:2], flat[2:4]]
    gate_ps, up_ps = flat[0:2], flat[2:4]
    scores_ps = flat[0:2]
    probsT_ps = flat[2:4]
    proj_ps = [down_ps[:, 0, :], down_ps[:, 1, :]]
    ctx_ps = down_ps[:, 2, :]
    y_ps = down_ps[:, 3, 0:D]

    x_in = [sem(f"x_in{b}") for b in range(B)]
    const_in = sem("const_in")
    raw_in = [sem(f"raw_in{i}") for i in range(RAW_SLOTS)]
    ffn_hi, ffn_split, attn_hi, attn_split = sem("ffn_hi"), sem("ffn_split"), sem("attn_hi"), sem("attn_split")
    stats_done, aggr_done, var_made, rstd_made = sem("stats_done"), sem("aggr_done"), sem("var_made"), sem("rstd_made")
    xn_made, xT_done, xT_hi, xT_split = sem("xn_made"), sem("xT_done"), sem("xT_hi"), sem("xT_split")
    gate_done, up_done, gate_silu, hid_made, hid_hi, hid_split = (
        sem("gate_done"), sem("up_done"), sem("gate_silu"), sem("hid_made"), sem("hid_hi"), sem("hid_split"))
    down_done, g_made, g_stored = sem("down_done"), sem("g_made"), sem("g_stored")
    g_free = sem("g_free")
    proj_done, proj_hi, proj_split = sem("proj_done"), sem("proj_hi"), sem("proj_split")
    scores_done, masked, exp_done, inv_made, probs_made = (
        sem("scores_done"), sem("masked"), sem("exp_done"), sem("inv_made"), sem("probs_made"))
    probsT_done, probsT_hi, probsT_split = sem("probsT_done"), sem("probsT_hi"), sem("probsT_split")
    ctx_done, ctx_hi, ctx_split = sem("ctx_done"), sem("ctx_hi"), sem("ctx_split")
    y_done, y_added = sem("y_done"), sem("y_added")
    x_b_in, g_b_in, xn_b_made, gelu_done, res_made = (
        sem("x_b_in"), sem("g_b_in"), sem("xn_b_made"), sem("gelu_done"), sem("res_made"))
    stats3_done, aggr3_done, var3_made, rstd3_made, z_made, out_made, out_stored, pool_chain = (
        sem("stats3_done"), sem("aggr3_done"), sem("var3_made"), sem("rstd3_made"), sem("z_made"),
        sem("out_made"), sem("out_stored"), sem("pool_chain"))
    consts_set = sem("consts_set")

    wgu_v = wgu.rearrange("(c p) (g n) -> p c g n", p=P, g=2)
    wd_v = wd.rearrange("(c p) n -> p c n", p=P)
    wq_v = wq.rearrange("(c p) n -> p c n", p=P)
    wk_v = wk.rearrange("(c p) n -> p c n", p=P)
    wv_v = wv.rearrange("(c p) n -> p c n", p=P)
    wo_v = wo.rearrange("(h p) n -> p h n", p=P)
    half = F // 2
    pieces = []

    def gate_up_cols(w, lo, c):
        return w[:, c, :].rearrange("p (g n) -> p g n", g=2)[:, :, lo:lo + half]

    for lo in (0, half):
        pieces.append([(wgu_v[:, c, :, lo:lo + half], (c * 2 * half, 2 * half, 2),
                        [gate_up_cols(w, lo, c) for w in wgu_s]) for c in range(DC)])
        if lo == 0:
            pieces.append([(wd_v, (0, FC * D, FC), [w[:, :, :] for w in wd_s])])
    pieces.append([(wk_v, (0, DC * KV * E, DC), [w[:, :, :] for w in wk_s]),
                   (wv_v, (DC * KV * E, DC * KV * E, DC), [w[:, :, :] for w in wv_s])])
    for c in range(DC):
        pieces.append([(wq_v[:, c:c + 1, :], (0, H * E, 1), [w[:, c:c + 1, :] for w in wq_s])])
    for i in range(2):
        hs = slice(i * H // 2, (i + 1) * H // 2)
        pieces.append([(wo_v[:, hs, :], (0, H // 2 * D, H // 2), [w[:, hs, :] for w in wo_s])])
    FFN_PIECES = 3
    FFN_PARTS = sum(len(p) for p in pieces[:FFN_PIECES])
    ALL_PARTS = sum(len(p) for p in pieces)

    def raw_view(k, at):
        start, width, n = at
        return raw[k % RAW_SLOTS][:, start:start + width].rearrange("p (a n) -> p a n", a=n)

    def parts():
        n = 0
        for k, piece in enumerate(pieces):
            for _, at, dst in piece:
                yield n, k, at, dst
                n += 1

    def landed(eng, k):
        eng.wait_ge(raw_in[k % RAW_SLOTS], 16 * len(pieces[k]) + 16 * sum(
            len(pieces[i]) for i in range(k % RAW_SLOTS, k, RAW_SLOTS)))

    block = ctx.enter_context(nc.Block())

    @block.sync
    def _(sp):
        def load_piece(k):
            for src, at, _ in pieces[k]:
                sp.dma_start(raw_view(k, at), src).then_inc(raw_in[k % RAW_SLOTS], 16)

        def load_tokens(b):
            sp.dma_start(x_all[:, b], x_v[b]).then_inc(x_in[b], 16)

        load_tokens(0)
        load_tokens(1)
        sp.dma_start(ident[:], ident_in).then_inc(const_in, 16)
        load_piece(0)
        load_tokens(2)
        load_tokens(3)
        load_piece(1)
        sp.dma_start(mask[:], mask_in).then_inc(const_in, 16)
        sp.dma_start(bias[:], bqkv).then_inc(const_in, 16)
        sp.dma_start(rowc[:], rows).then_inc(const_in, 16)
        done_parts = 0
        for k in range(RAW_SLOTS, len(pieces)):
            done_parts += len(pieces[k - RAW_SLOTS])
            if k - RAW_SLOTS < FFN_PIECES:
                sp.wait_ge(ffn_split, done_parts)
            else:
                sp.wait_ge(attn_split, done_parts - FFN_PARTS)
            load_piece(k)
        sp.sem_inc(g_free, 1)
        for b in range(B):
            sp.wait_ge(g_made, b + 1)
            sp.dma_start(g_v[b], g_out[:]).then_inc(g_stored, 16)
            sp.wait_ge(g_stored, 16 * b + 16)
            sp.sem_inc(g_free, 1)
        sp.wait_ge(down_done, B)
        for b in range(B):
            sp.dma_start(x_b[:], x_v[b]).then_inc(x_b_in, 16)
            sp.dma_start(g_b[:], g_v[b]).then_inc(g_b_in, 16)
            sp.wait_ge(out_made, b + 1)
            sp.dma_start(out_v[b], res[:]).then_inc(out_stored, 16)
            sp.wait_ge(out_stored, 16 * b + 16)

    @block.gpsimd
    def _(pool):
        nc.gpsimd.memset(neghalf[:], -0.5).then_inc(pool_chain, 1)
        pool.wait_ge(pool_chain, 1)
        pool.wait_ge(var_made, 1)
        nc.gpsimd.tensor_tensor(norm[:, :, 1], ve1[:], neghalf[:], ALU.pow).then_inc(rstd_made, 1)
        for n, k, at, (hi, lo) in parts():
            if k >= FFN_PIECES:
                landed(pool, k)
                nc.gpsimd.tensor_copy(hi, raw_view(k, at)).then_inc(attn_hi, 1)
                pool.wait_ge(attn_hi, n - FFN_PARTS + 1)
                nc.gpsimd.tensor_tensor(lo, raw_view(k, at), f32(hi), ALU.subtract).then_inc(attn_split, 1)

        def over_tiles(row):
            return row.rearrange("p (a n) -> p a n", a=1).to_broadcast([P, T, D])

        def residual(b):
            pool.wait_ge(gelu_done, b + 1)
            pool.wait_ge(xn_b_made, b + 1)
            nc.gpsimd.tensor_tensor(res[:], res[:], xn_b[:], ALU.add).then_inc(res_made, 1)

        def root(b):
            pool.wait_ge(var3_made, b + 1)
            nc.gpsimd.tensor_tensor(rstd3[:], ve3[:], neghalf[:, 0:T], ALU.pow).then_inc(rstd3_made, 1)

        def output(b):
            pool.wait_ge(z_made, b + 1)
            pool.wait_ge(g_b_in, 16 * b + 16)
            for i, (other, op) in enumerate(((over_tiles(gamma_row), ALU.mult), (over_tiles(beta_row), ALU.add),
                                             (g_b[:], ALU.mult))):
                nc.gpsimd.tensor_tensor(res[:], res[:], other, op).then_inc(pool_chain, 1)
                pool.wait_ge(pool_chain, b * 3 + 2 + i)
            nc.gpsimd.tensor_tensor(res[:], res[:], x_b[:], ALU.add).then_inc(out_made, 1)

        def steps(b, order, ends=()):
            done = 0
            for step in order:
                if step[0] == "s":
                    _, u, g = step
                    pool.wait_ge(inv_made, b * SCORES_ALL + u * G + g + 1)
                    p = probs[tile_of(u)][:, g, :]
                    nc.gpsimd.tensor_tensor(p, p, inv[:, u % UNITS, g:g + 1].to_broadcast([P, (tile_of(u) + 1) * P]),
                                            ALU.mult).then_inc(probs_made, 1)
                    done += 1
                for at, work in ends:
                    if step[0] == "s" and done == at:
                        work(b)

        steps(0, segment(-1, text=AHEAD))
        steps(0, segment(0))
        with pool.Fori(0, B - 1) as b:
            for kv in range(1, KV):
                steps(b, segment(kv))
            steps(b, segment(KV), ((G, residual), (2 * G, root), (2 * G, output)))
        for kv in range(1, KV):
            steps(B - 1, segment(kv, last=kv == KV - 1))
        for work in (residual, root, output):
            work(B - 1)

    @block.scalar
    def _(act):
        def weight_hi(piece):
            for n, k, at, (hi, lo) in parts():
                if k == piece:
                    landed(act, k)
                    nc.scalar.activation(hi, raw_view(k, at), ACT.Copy).then_inc(ffn_hi, 1)

        for b in range(B):
            for c in range(DC):
                act.wait_ge(xT_done, b * DC + c + 1)
                nc.scalar.activation(xnT[0][:, c, b * L:(b + 1) * L], xT_ps[b % 2][c], ACT.Copy).then_inc(xT_hi, 1)
            if b == 1:
                weight_hi(0)
        weight_hi(1)
        weight_hi(2)

        with act.Fori(0, B) as b:
            for c in range(FC):
                act.wait_ge(gate_done, b * FC + c + 1)
                nc.scalar.activation(gate[:, c % 2], gate_ps[c % 2], ACT.Silu).then_inc(gate_silu, 1)
                act.wait_ge(hid_made, b * FC + c + 1)
                nc.scalar.activation(hidT[c % 2][0][:], hid[:, c % 2], ACT.Copy).then_inc(hid_hi, 1)
            act.wait_ge(g_free, b + 1)
            act.wait_ge(down_done, b + 1)
            nc.scalar.activation(g_out[:], down_ps[:, :, 0:D], ACT.Silu).then_inc(g_made, 1)

        def gelu(b):
            act.wait_ge(x_b_in, 16 * b + 16)
            act.wait_ge(y_added, b * UNITS + UNITS)
            nc.scalar.activation(res[:], y[:], ACT.Gelu).then_inc(gelu_done, 1)

        def steps(b, order, gelu_behind=None):
            for step in order:
                if step[0] in "kwq":
                    n = proj_index(step)
                    kv = step[1] % KV
                    act.wait_ge(proj_done, b * PROJ_ALL + n + 1)
                    if step[0] == "k":
                        nc.scalar.activation(kT[0][:], proj_ps[n % 2], ACT.Identity,
                                             bias=bias[:, H + kv:H + kv + 1]).then_inc(proj_hi, 1)
                    elif step[0] == "q":
                        h = step[2] * KV + kv
                        nc.scalar.activation(qT[step[2]][0][:], proj_ps[n % 2], ACT.Identity,
                                             bias=bias[:, h:h + 1]).then_inc(proj_hi, 1)
                    else:
                        nc.scalar.activation(v_s[kv % 2][0][:].rearrange("p t e -> p (t e)"), proj_ps[n % 2],
                                             ACT.Copy).then_inc(proj_hi, 1)
                elif step[0] == "s":
                    _, u, g = step
                    p = probs[tile_of(u)][:, g, :]
                    act.wait_ge(masked, b * SCORES_ALL + u * G + g + 1)
                    nc.scalar.activation(p, p, ACT.Exp, bias=least[:, u % UNITS, g:g + 1], scale=-1.0,
                                         accum_out=total[:, u % UNITS, g:g + 1]).then_inc(exp_done, 1)
                elif step[0] == "t":
                    r = pair_index(*step[1:])
                    act.wait_ge(probsT_done, b * PAIRS + r + 1)
                    nc.scalar.activation(pT[r % 2][0][:], probsT_ps[r % 2], ACT.Copy).then_inc(probsT_hi, 1)
                elif step[0] == "p" and step[2] == tile_of(step[1]):
                    act.wait_ge(ctx_done, b * UNITS + step[1] + 1)
                    nc.scalar.activation(cT[0][:], ctx_ps, ACT.Copy).then_inc(ctx_hi, 1)
                if step == gelu_behind:
                    gelu(b)

        steps(0, segment(-1, text=AHEAD))
        steps(0, segment(0))
        with act.Fori(0, B - 1) as b:
            for kv in range(1, KV):
                steps(b, segment(kv))
            steps(b, segment(KV), gelu_behind=("t", KV * T, 1))
        for kv in range(1, KV):
            steps(B - 1, segment(kv, last=kv == KV - 1))
        gelu(B - 1)

    @block.vector
    def _(dve):
        for b in range(B):
            dve.wait_ge(x_in[b], 16)
            for t in range(T):
                last = nc.vector.bn_stats(stats1[:, b * T + t, :], x_all[:, b, t, :])
        last.then_inc(stats_done, 1)
        dve.wait_ge(stats_done, 1)
        for t in range(B * T):
            last = nc.vector.bn_aggr(norm[:, t, :], stats1[:, t, :])
        last.then_inc(aggr_done, 1)
        dve.wait_ge(aggr_done, 1)
        nc.vector.tensor_scalar(ve1[:], norm[:, :, 1], EPS, None, ALU.add).then_inc(var_made, 1)
        dve.wait_ge(rstd_made, 1)

        def normalise(b):
            for t in range(T):
                last = nc.vector.tensor_scalar(xn[:, b % 2, t, :], x_all[:, b, t, :], norm[:, b * T + t, 0:1],
                                               norm[:, b * T + t, 1:2], ALU.subtract, ALU.mult)
            last.then_inc(xn_made, 1)

        def xT_low(b):
            for c in range(DC):
                dve.wait_ge(xT_hi, b * DC + c + 1)
                part = [w[:, c, b * L:(b + 1) * L] for w in xnT]
                nc.vector.tensor_tensor(part[1], xT_ps[b % 2][c], f32(part[0]), ALU.subtract).then_inc(xT_split, 1)

        def weight_low(piece):
            for n, k, at, (hi, lo) in parts():
                if k == piece:
                    dve.wait_ge(ffn_hi, n + 1)
                    nc.vector.tensor_tensor(lo, raw_view(k, at), f32(hi), ALU.subtract).then_inc(ffn_split, 1)

        normalise(0)
        normalise(1)
        xT_low(0)
        normalise(2)
        xT_low(1)
        normalise(3)
        weight_low(0)
        xT_low(2)
        xT_low(3)
        weight_low(1)
        weight_low(2)

        with dve.Fori(0, B) as b:
            for c in range(FC):
                dve.wait_ge(up_done, b * FC + c + 1)
                dve.wait_ge(gate_silu, b * FC + c + 1)
                nc.vector.tensor_tensor(hid[:, c % 2], gate[:, c % 2], up_ps[c % 2], ALU.mult).then_inc(hid_made, 1)
                dve.wait_ge(hid_hi, b * FC + c + 1)
                nc.vector.tensor_tensor(hidT[c % 2][1][:], hid[:, c % 2], f32(hidT[c % 2][0][:]),
                                        ALU.subtract).then_inc(hid_split, 1)

        def low_part(step, b):
            if step[0] == "t":
                r = pair_index(*step[1:])
                dve.wait_ge(probsT_hi, b * PAIRS + r + 1)
                hi, lo = pT[r % 2]
                nc.vector.tensor_tensor(lo[:], probsT_ps[r % 2], f32(hi[:]), ALU.subtract).then_inc(probsT_split, 1)
            elif step[0] in "kwq":
                n = proj_index(step)
                kv = step[1] % KV
                taken = n - (step[1] + (step[0] != "k")) + 1
                dve.wait_ge(proj_hi, b * (PROJ_ALL - KV) + taken)
                if step[0] == "w":
                    hi, lo = (w[:].rearrange("p t e -> p (t e)") for w in v_s[kv % 2])
                    nc.vector.tensor_tensor(lo, proj_ps[n % 2], f32(hi), ALU.subtract).then_inc(proj_split, 1)
                else:
                    h = H + kv if step[0] == "k" else step[2] * KV + kv
                    hi, lo = kT if step[0] == "k" else qT[step[2]]
                    nc.vector.scalar_tensor_tensor(lo[:], proj_ps[n % 2], bias[:, h:h + 1], f32(hi[:]),
                                                   ALU.add, ALU.subtract).then_inc(proj_split, 1)
            else:
                dve.wait_ge(ctx_hi, b * UNITS + step[1] + 1)
                hi, lo = cT
                nc.vector.tensor_tensor(lo[:], ctx_ps, f32(hi[:]), ALU.subtract).then_inc(ctx_split, 1)

        def xn_again(b):
            dve.wait_ge(x_b_in, 16 * b + 16)
            for t in range(T):
                at = norm[:, bass.ds(b * T + t, 1), :]
                last = nc.vector.tensor_scalar(xn_b[:, t, :], x_b[:, t, :], at[:, 0, 0:1], at[:, 0, 1:2],
                                               ALU.subtract, ALU.mult)
            last.then_inc(xn_b_made, 1)

        def statistics(b):
            dve.wait_ge(res_made, b + 1)
            for t in range(T):
                last = nc.vector.bn_stats(stats3[:, t, :], res[:, t, :])
            last.then_inc(stats3_done, 1)
            dve.wait_ge(stats3_done, b + 1)
            nc.vector.memset(ve3[:], EPS)
            for t in range(T):
                last = nc.vector.bn_aggr(mv3[:, t, :], stats3[:, t, :])
            last.then_inc(aggr3_done, 1)
            dve.wait_ge(aggr3_done, b + 1)
            nc.vector.tensor_tensor(ve3[:], mv3[:, :, 1], ve3[:], ALU.add).then_inc(var3_made, 1)

        def norm_again(b):
            dve.wait_ge(rstd3_made, b + 1)
            for t in range(T):
                last = nc.vector.tensor_scalar(res[:, t, :], res[:, t, :], mv3[:, t, 0:1], rstd3[:, t:t + 1],
                                               ALU.subtract, ALU.mult)
            last.then_inc(z_made, 1)

        def steps(b, order, ends=()):
            for step in vector_steps(order):
                if step[0] == "masked":
                    _, u, g = step
                    t = tile_of(u)
                    n = u * G + g
                    dve.wait_ge(scores_done, b * SCORES_ALL + n + 1)
                    nc.vector.memset(total[:, u % UNITS, g:g + 1], 0.0)
                    nc.vector.tensor_tensor_reduce(
                        out=probs[t][:, g, :], in0=scores_ps[n % 2][:, 0:(t + 1) * P],
                        in1=mask[:, (T - 1 - t) * P:], scale=-SCALE, scalar=BIG, op0=ALU.add, op1=ALU.min,
                        accum_out=least[:, u % UNITS, g:g + 1]).then_inc(masked, 1)
                elif step[0] == "inv":
                    _, u, g = step
                    dve.wait_ge(exp_done, b * SCORES_ALL + u * G + g + 1)
                    nc.vector.reciprocal(inv[:, u % UNITS, g:g + 1], total[:, u % UNITS, g:g + 1]).then_inc(inv_made, 1)
                elif step[0] == "low":
                    low_part(step[1], b)
                elif step[0] == "v":
                    n = proj_index(step)
                    dve.wait_ge(proj_done, b * PROJ_ALL + n + 1)
                    h = H + KV + step[1] % KV
                    nc.vector.tensor_scalar(vT[:], proj_ps[n % 2], bias[:, h:h + 1], None,
                                            ALU.add).then_inc(proj_split, 1)
                else:
                    u = step[1]
                    t = tile_of(u)
                    dve.wait_ge(y_done, b * UNITS + u + 1)
                    base = bo_row if kv_of(u) % KV == 0 else y[:, t, :]
                    nc.vector.tensor_tensor(y[:, t, :], y_ps, base, ALU.add).then_inc(y_added, 1)
                for at, work in ends:
                    if step == at:
                        work(b)

        def low_of(kv, *step):
            return "low", (step[0], kv, *step[1:])

        steps(0, segment(-1, text=AHEAD))
        steps(0, segment(0))
        with dve.Fori(0, B - 1) as b:
            for kv in range(1, KV):
                steps(b, segment(kv), ((low_of(kv + 1, "k"), xn_again),) if kv == KV - 1 else ())
            steps(b, segment(KV), ((low_of(KV + 1, "q", 0), statistics), (low_of(KV + 1, "q", 2), norm_again)))
        for kv in range(1, KV):
            steps(B - 1, segment(kv, last=kv == KV - 1), ((("masked", (KV - 1) * T + T - 1, 0), xn_again),) if kv == KV - 1 else ())
        statistics(B - 1)
        norm_again(B - 1)

    @block.tensor
    def _(pe):
        def product(dst, left, right, first, last):
            for i, (a, c) in enumerate(PASSES):
                ins = nc.tensor.matmul(dst, left[a], right[c], start=first and i == 0,
                                       stop=last and i == len(PASSES) - 1)
            return ins

        pe.wait_ge(const_in, 64)
        for b in range(B):
            pe.wait_ge(xn_made, b + 1)
            if b >= 2:
                pe.wait_ge(xT_split, (b - 1) * DC)
            for c in range(DC):
                for t in range(T):
                    last = nc.tensor.transpose(xT_ps[b % 2][c][:, t * P:(t + 1) * P],
                                               xn[:, b % 2, t, c * P:(c + 1) * P], ident[:])
                last.then_inc(xT_done, 1)

        def gate_up(b, c):
            if c >= 2:
                pe.wait_ge(hid_made, b * FC + c - 1)
            if c in (0, FC // 2):
                pe.wait_ge(ffn_split, len(pieces[0]) if c == 0 else FFN_PARTS)
            for i, (ps, done) in enumerate(((gate_ps, gate_done), (up_ps, up_done))):
                at = i * F + c * P
                for k in range(DC):
                    last = product(ps[c % 2], [w[:, k, at:at + P] for w in wgu_s],
                                   [w[:, k, bass.ds(b * L, L)] for w in xnT], k == 0, k == DC - 1)
                last.then_inc(done, 1)

        def down(b, c):
            if c == 0:
                pe.wait_ge(ffn_split, len(pieces[0]) + len(pieces[1]))
            pe.wait_ge(hid_split, b * FC + c + 1)
            for t in range(T):
                last = product(down_ps[:, t, 0:D], [w[:, t * P:(t + 1) * P] for w in hidT[c % 2]],
                               [w[:, c, :] for w in wd_s], c == 0, c == FC - 1)
            return last

        pe.wait_ge(xT_split, B * DC)
        with pe.Fori(0, B) as b:
            for c in range(FC):
                gate_up(b, c)
                if c:
                    down(b, c - 1)
            down(b, FC - 1).then_inc(down_done, 1)

        def project(b, step):
            kind, kv = step[0], step[1]
            n = proj_index(step)
            if n >= 2:
                pe.wait_ge(proj_split, b * PROJ_ALL + n - 1)
            if kind == "w":
                pe.wait_ge(proj_split, b * PROJ_ALL + proj_index(("v", kv)) + 1)
                for j in range(T):
                    last = nc.tensor.transpose(proj_ps[n % 2][:, j * P:(j + 1) * P], vT[:, j * P:(j + 1) * P], ident[:])
            else:
                w_s = {"k": wk_s, "v": wv_s, "q": wq_s}[kind]
                at = (step[2] * KV + kv % KV if kind == "q" else kv % KV) * E
                row = b + kv // KV
                for c in range(DC):
                    last = product(proj_ps[n % 2], [w[:, c, at:at + E] for w in w_s],
                                   [w[:, c, bass.ds(row * L, L)] for w in xnT], c == 0, c == DC - 1)
            last.then_inc(proj_done, 1)

        def scores(b, u, g):
            n = u * G + g
            t = tile_of(u)
            pe.wait_ge(proj_split, b * PROJ_ALL + proj_index(("q", kv_of(u), g)) + 1)
            if n >= 2:
                pe.wait_ge(masked, b * SCORES_ALL + n - 1)
            width = max(2, t + 1) * P
            product(scores_ps[n % 2][:, 0:width], [w[:, t * P:(t + 1) * P] for w in qT[g]],
                    [w[:, 0:width] for w in kT], True, True).then_inc(scores_done, 1)

        def transposes(b, u, j):
            r = pair_index(u, j)
            if j == 0:
                pe.wait_ge(probs_made, b * SCORES_ALL + (u + 1) * G)
            if r >= 2:
                pe.wait_ge(probsT_split, b * PAIRS + r - 1)
            for g in range(G):
                last = nc.tensor.transpose(probsT_ps[r % 2][:, g * P:(g + 1) * P],
                                           probs[tile_of(u)][:, g, j * P:(j + 1) * P], ident[:])
            last.then_inc(probsT_done, 1)

        def values(b, u, j):
            r = pair_index(u, j)
            pe.wait_ge(probsT_split, b * PAIRS + r + 1)
            if j == 0:
                pe.wait_ge(proj_split, b * PROJ_ALL + proj_index(("w", kv_of(u))) + 1)
                if u:
                    pe.wait_ge(ctx_split, b * UNITS + u)
            last = product(ctx_ps, [w[:, j, :] for w in v_s[kv_of(u) % 2]], [w[:] for w in pT[r % 2]],
                           j == 0, j == tile_of(u))
            if j == tile_of(u):
                last.then_inc(ctx_done, 1)

        def output(b, u):
            pe.wait_ge(ctx_split, b * UNITS + u + 1)
            if u:
                pe.wait_ge(y_added, b * UNITS + u)
            for g in range(G):
                last = product(y_ps, [w[:, g * P:(g + 1) * P] for w in cT], [w[:, g * KV + kv_of(u) % KV, :] for w in wo_s],
                               g == 0, g == G - 1)
            last.then_inc(y_done, 1)

        pe.wait_ge(attn_split, ALL_PARTS - FFN_PARTS)
        pe.wait_ge(g_made, B)
        def steps(b, order):
            for step in order:
                if step[0] in "kvwq":
                    project(b, step)
                elif step[0] == "s":
                    scores(b, *step[1:])
                elif step[0] == "t":
                    transposes(b, *step[1:])
                elif step[0] == "p":
                    values(b, *step[1:])
                else:
                    output(b, step[1])

        steps(0, segment(-1, text=AHEAD))
        steps(0, segment(0))
        with pe.Fori(0, B - 1) as b:
            for kv in range(1, KV):
                steps(b, segment(kv))
            steps(b, segment(KV))
        for kv in range(1, KV):
            steps(B - 1, segment(kv, last=kv == KV - 1))

    ctx.close()




def kernel(**inputs):
    import concourse.bacc as bacc
    from concourse.bass_utils import run_bass_kernel_spmd

    def get(name):
        return np.asarray(inputs["L0_" + name])

    def by_head(a):
        return a.reshape(-1, E).T

    keys = np.arange(P)
    mask = np.zeros((P, L), np.float32)
    mask[:, L - P:] = np.where(keys[None, :] > keys[:, None], np.float32(MASK), np.float32(0))
    arrays = {
        "x": get("attn_x"),
        "wq": get("attn_Wq"),
        "wk": get("attn_Wk"),
        "wv": get("attn_Wv"),
        "wo": get("attn_Wo"),
        "wgu": get("ffn_w_gate_up").T,
        "wd": get("ffn_w_down").T,
        "bqkv": np.concatenate([by_head(get("attn_bq")), by_head(get("attn_bk")), by_head(get("attn_bv"))], axis=1),
        "rows": np.broadcast_to(np.stack([get("attn_bo"), get("attn_gamma"), get("attn_beta")]), (P, 3, D)),
        "ident": np.eye(P, dtype=np.float32),
        "mask": mask,
    }
    arrays = {f"in_{k}": np.ascontiguousarray(v) for k, v in arrays.items()}
    nc = bacc.Bacc("TRN2", target_bir_lowering=False, num_devices=1)
    args = [nc.dram_tensor(k, a.shape, F32, kind="ExternalInput").ap() for k, a in arrays.items()]
    g_scratch = nc.dram_tensor("g_scratch", (B, L, D), F32, kind="Internal").ap()
    out = nc.dram_tensor("out", (B, L, D), F32, kind="ExternalOutput").ap()
    build(nc, *args, g_scratch, out)
    r = run_bass_kernel_spmd(nc, [arrays], core_ids=[0])
    return r.results[0]["out"]
```

```python
import math
from contextlib import ExitStack

import numpy as np

import concourse.bass as bass
from concourse import mybir

F32 = mybir.dt.float32
F32R = mybir.dt.float32r
ALU = mybir.AluOpType
ACT = mybir.ActivationFunctionType

P = 128
B, L, D = 4, 512, 256
H, KV, E = 16, 4, 128
G = H // KV
F = 1024
DC = D // P
FC = F // P
T = L // P
EPS = 1e-5
SCALE = 1.0 / math.sqrt(E)
MASK = -1e9 / SCALE
BIG = 3.0e38
PASSES = ((0, 1), (1, 0), (0, 0))

PIECE = 2048
RAW_SLOTS = 2

MASK_LAG = (0, 0, 1, 1)
EXP_LAG = (6, 3, 3, 2)
INVERSE_LAG = (7, 6, 7, 3)

SEGMENT = """
s1.0 t3.0 o s1.1 t3.1 s1.2 p3.0 t3.2 s1.3 s0.0 p3.1 t3.3 s0.1 p3.2 s0.2
t2.0 s0.3 p3.3 V t2.1 K p2.0 o t2.2 Q0 W Q1 Q2 p2.1
t1.0 p2.2 t1.1 S3.0 Q3 p1.0 S3.1 o p1.1
t0.0 S3.2 S3.3 o S2.0 S2.1 S2.2 p0.0 S2.3
"""
LAST_SEGMENT = """
s1.0 t3.0 o t3.1 s1.1 p3.0 t3.2 s1.2 s1.3 p3.1 s0.0 s0.1 t3.3 p3.2 s0.2 s0.3
t2.0 p3.3 t2.1 t2.2 p2.0
t1.0 p2.1 o p2.2 t1.1
t0.0 p1.0 o p1.1 o p0.0
"""
ROW_END_ACT = (("gelu", "s0.0"),)
ROW_END_DVE = (("statistics", "t2.1"), ("norm", "t2.2"))
ROW_END_POOL = (("residual", "s1.3"), ("root", "s0.0"), ("out0", "s0.3"), ("out1", "s0.3"), ("out2", "s0.3"),
                ("out3", "s0.3"), ("out4", "s0.3"), ("out5", "s0.3"), ("out6", "S3.0"), ("out7", "S2.0"))
LAST_ACT = (("gelu", 3, "t0.0"), ("gelu", 2, "p1.1"), ("gelu", 1, "p0.0"))
LAST_DVE = (("output", 3, "p1.1"), ("statistics", 3, "t0.0"), ("statistics", 2, "p1.1"), ("statistics", 1, "p0.0"))
FIRST = "V K Q0"
AHEAD = "W Q1 Q2 Q3 S3.0 S3.1 S3.2 S3.3 S2.0 S2.1 S2.2 S2.3"
UNITS = KV * T
LAST = (KV - 1) * T
PROJ = [w for w in SEGMENT.split() if w[0] in "KVWQ"]
PROJ_OF_KV = len(PROJ)
PROJ_ALL = KV * PROJ_OF_KV
PAIRS_OF_KV = T * (T + 1) // 2
PAIRS = KV * PAIRS_OF_KV
SCORES_ALL = UNITS * G
RING_BANKS = 4
assert KV * (PROJ_OF_KV + T * G) % RING_BANKS == 0


def kv_of(u):
    return u // T


def tile_of(u):
    return T - 1 - u % T


def segment(kv, last=False, text=None):
    pending = kv * T - 1
    for word in (text or (LAST_SEGMENT if last else SEGMENT)).split():
        kind, rest = word[0].lower(), word[1:]
        of = kv + 1 if word[0] in "KVWQS" else kv
        if kind == "q":
            yield kind, of, int(rest)
        elif kind in "kvw":
            yield kind, of
        elif kind == "o":
            if pending >= 0:
                yield kind, pending
            pending += 1
        else:
            t, i = map(int, rest.split("."))
            yield kind, of * T + T - 1 - t, i
    if last:
        yield "o", pending


def behind_word(ends, works, b, step):
    for name, word in ends:
        if step == next(segment(KV, text=word)):
            works[name](b)


def works_behind(table, works, step):
    for name, tile, word in table:
        if word[0] == "o":
            place = "o", LAST - 1 + int(word[1:])
        else:
            place = next(segment(KV - 1, text=word))
        if step == place:
            works[name](LAST + T - 1 - tile)


def pair_place(step, end):
    r = pair_index(*step[1:])
    spare = r - (KV - 1) * PAIRS_OF_KV - (PAIRS_OF_KV - G)
    return (True, spare) if end and spare >= 0 else (False, r % 2)


def proj_index(step):
    return step[1] * PROJ_OF_KV + PROJ.index(step[0].upper() + "".join(map(str, step[2:])))


def highs_done(step):
    return step[1] * (PROJ_OF_KV - 1) + sum(w != "V" for w in PROJ[:proj_index(step) % PROJ_OF_KV + 1])


def ring(last=False):
    steps = [*segment(-1, text=FIRST), *segment(-1, text=AHEAD)]
    for kv in range(KV - 1 if last else KV + 1):
        steps += segment(kv)
    if last:
        steps += segment(KV - 1, last=True)
    uses = [x for x in steps if x[0] in "kvwqs"]
    return {x: (i % RING_BANKS, uses[i - RING_BANKS] if i >= RING_BANKS else None)
            for i, x in enumerate(uses)}


def pair_index(u, j):
    return kv_of(u) * PAIRS_OF_KV + sum(tile + 1 for tile in range(tile_of(u) + 1, T)) + j


def behind(steps, lag, i):
    for j, x in enumerate(steps[:i + 1]):
        if x[0] == "s":
            turn = min(j + lag[tile_of(x[1])], len(steps))
            if turn == i:
                yield x


def scalar_steps(steps):
    steps = list(steps)
    for i in range(len(steps) + 1):
        yield from behind(steps, EXP_LAG, i)
        if i < len(steps) and steps[i][0] != "s":
            yield steps[i]


def vector_steps(steps):
    steps = list(steps)
    for i in range(len(steps) + 1):
        step = steps[i] if i < len(steps) else ("end",)
        masked = [("masked", *x[1:]) for x in behind(steps, MASK_LAG, i)]
        if step[0] == "s" and ("masked", *step[1:]) in masked:
            masked.remove(("masked", *step[1:]))
            yield "masked", *step[1:]
        before = steps[i - 1] if i else ("start",)
        if before[0] in ("k", "w", "q", "t") or before[0] == "p" and before[2] == tile_of(before[1]):
            yield "low", before
        yield from masked
        yield from (("inv", *x[1:]) for x in behind(steps, INVERSE_LAG, i))
        if step[0] in ("v", "o"):
            yield step


def build(nc, x, wq, wk, wv, wo, wgu, wd, bqkv, rows, ident_in, mask_in, g_scratch, out):
    ctx = ExitStack()

    def sb(name, shape, dt=F32, stack=ctx):
        return stack.enter_context(nc.sbuf_tensor(name, shape, dt))

    def pb(name, shape, stack=ctx):
        return stack.enter_context(nc.psum_tensor(name, shape, F32))

    def sem(name):
        return ctx.enter_context(nc.semaphore(name))

    def pair(name, shape, stack=ctx):
        return [sb(f"{name}_{part}", shape, F32R, stack) for part in ("hi", "lo")]

    def f32(ap):
        return ap.bitcast(F32)

    x_v = x.rearrange("b (t p) d -> b p t d", p=P)
    out_v = out.rearrange("b (t p) d -> b p t d", p=P)
    g_v = g_scratch.rearrange("b (t p) d -> b p t d", p=P)

    wq_s = pair("wq", [P, DC, H * E])
    wk_s = pair("wk", [P, DC, KV * E])
    wv_s = pair("wv", [P, DC, KV * E])
    wo_s = pair("wo", [P, H, D])
    xnT = pair("xnT", [P, DC, B * L])
    norm = sb("norm", [P, B * T, 2])
    bias = sb("bias", [P, H + 2 * KV])
    rowc = sb("rowc", [P, 3, D])
    ident = sb("ident", [P, P])
    mask = sb("mask", [P, L])
    neghalf = sb("neghalf", [P, T])
    warm = sb("warm", [P, 1])
    bo_row, gamma_row, beta_row = (rowc[:, i, :] for i in range(3))

    early = ExitStack()
    wgu_s = pair("wgu", [P, DC, 2 * F], early)
    wd_s = pair("wd", [P, FC, D], early)
    raw = [sb(f"raw{i}", [P, PIECE], F32, early) for i in range(RAW_SLOTS)]
    first = ExitStack()
    xn = sb("xn", [P, 2, T, D], F32, first)
    x_row = [sb(f"x_row{b}", [P, T, D], F32, first) for b in range(B)]
    stats1 = sb("stats1", [P, B * T, 6], F32, first)
    ve1 = sb("ve1", [P, B * T], F32, first)
    first.close()
    hidT = [pair(f"hidT{i}", [P, L], early) for i in range(2)]
    gate = sb("gate", [P, 2, L], F32, early)
    hid = sb("hid", [P, 2, L], F32, early)
    g_out = sb("g_out", [P, T, D], F32, early)
    early.close()

    qT = [pair(f"qT{g}", [P, L]) for g in range(G)]
    kT = pair("kT", [P, L])
    q_first = sb("q_first", [P, G, P])
    k_first = sb("k_first", [P, P])
    vT = sb("vT", [P, L])
    v_s = [pair(f"v{i}", [P, T, E]) for i in range(2)]
    probs = [sb(f"probs{t}", [P, G, (t + 1) * P]) for t in range(T)]
    pT = [pair(f"pT{i}", [P, G * P]) for i in range(2)]
    cT = pair("cT", [P, G * P])
    y = sb("y", [P, T, D])
    least = sb("least", [P, UNITS, G])
    total = sb("total", [P, UNITS, G])
    inv = sb("inv", [P, UNITS, G])
    x_b = sb("x_b", [P, T, D])
    g_b = sb("g_b", [P, T, D])
    xn_b = sb("xn_b", [P, T, D])
    res = sb("res", [P, T, D])
    stats3 = sb("stats3", [P, T, 6])
    mv3 = sb("mv3", [P, T, 2])
    ve3 = sb("ve3", [P, T])
    rstd3 = sb("rstd3", [P, T])

    bank = [pb(f"bank{i}", [P, 4, P]) for i in range(4)]
    down_ps = pb("down_ps", [P, T, L])
    flat = [b[:].rearrange("p a n -> p (a n)") for b in bank]
    xT_ps = [flat[0:2], flat[2:4],
             [down_ps[:, 0, :], down_ps[:, 1, :]], [down_ps[:, 2, :], down_ps[:, 3, :]]]
    gate_ps, up_ps = flat[0:2], flat[2:4]
    ring_ps = flat
    probsT_ps = [down_ps[:, 0, :], down_ps[:, 1, :]]
    ctx_ps = down_ps[:, 2, :]
    y_ps = down_ps[:, 3, 0:D]

    def transposed(step, end):
        spare, slot = pair_place(step, end)
        return (ring_ps[slot], qT[slot]) if spare else (probsT_ps[slot], pT[slot])

    x_in = [sem(f"x_in{b}") for b in range(B)]
    ident_loaded, const_in = sem("ident_loaded"), sem("const_in")
    raw_in = [sem(f"raw_in{i}") for i in range(RAW_SLOTS)]
    attn_in = [sem(f"attn_in{i}") for i in range(RAW_SLOTS)]
    ffn_hi, ffn_split_dve, ffn_split_pool = sem("ffn_hi"), sem("ffn_split_dve"), sem("ffn_split_pool")
    attn_hi, attn_split = sem("attn_hi"), sem("attn_split")
    stats_done, aggr_done, var_made, rstd_made = (
        sem("stats_done"), sem("aggr_done"), sem("var_made"), sem("rstd_made"))
    xn_made, xT_done, xT_hi, xT_split = sem("xn_made"), sem("xT_done"), sem("xT_hi"), sem("xT_split")
    gate_done, up_done, gate_silu, hid_made, hid_hi, hid_split = (
        sem("gate_done"), sem("up_done"), sem("gate_silu"), sem("hid_made"), sem("hid_hi"), sem("hid_split"))
    down_done, g_made, g_stored = sem("down_done"), sem("g_made"), sem("g_stored")
    g_free = sem("g_free")
    proj_done, proj_hi, proj_split = sem("proj_done"), sem("proj_hi"), sem("proj_split")
    scores_done, masked, exp_done, inv_made, probs_made = (
        sem("scores_done"), sem("masked"), sem("exp_done"), sem("inv_made"), sem("probs_made"))
    probsT_done, probsT_hi, probsT_split = sem("probsT_done"), sem("probsT_hi"), sem("probsT_split")
    ctx_done, ctx_hi, ctx_split = sem("ctx_done"), sem("ctx_hi"), sem("ctx_split")
    y_done, y_added = sem("y_done"), sem("y_added")
    x_b_in, g_b_in, xn_b_made, gelu_done, res_made = (
        sem("x_b_in"), sem("g_b_in"), sem("xn_b_made"), sem("gelu_done"), sem("res_made"))
    stats3_done, aggr3_done, var3_made, rstd3_made, z_made, out_made, out_stored, pool_chain = (
        sem("stats3_done"), sem("aggr3_done"), sem("var3_made"), sem("rstd3_made"), sem("z_made"),
        sem("out_made"), sem("out_stored"), sem("pool_chain"))
    table_warm = sem("table_warm")
    tile_gelu, tile_var, tile_root, tile_normed, tile_chain_pool, tile_chain_dve, tile_out_pool, tile_out_dve, tile_scaled = (
        sem("tile_gelu"), sem("tile_var"), sem("tile_root"), sem("tile_normed"), sem("tile_chain_pool"),
        sem("tile_chain_dve"), sem("tile_out_pool"), sem("tile_out_dve"), sem("tile_scaled"))

    wgu_v = wgu.rearrange("(c p) (g n) -> p c g n", p=P, g=2)
    wd_v = wd.rearrange("(c p) n -> p c n", p=P)
    wq_v = wq.rearrange("(c p) n -> p c n", p=P)
    wk_v = wk.rearrange("(c p) n -> p c n", p=P)
    wv_v = wv.rearrange("(c p) n -> p c n", p=P)
    wo_v = wo.rearrange("(h p) n -> p h n", p=P)
    half = F // 2
    pieces = []

    def gate_up_cols(w, lo, c):
        return w[:, c, :].rearrange("p (g n) -> p g n", g=2)[:, :, lo:lo + half]

    for lo in (0, half):
        pieces.append([(wgu_v[:, c, :, lo:lo + half], (c * 2 * half, 2 * half, 2),
                        [gate_up_cols(w, lo, c) for w in wgu_s]) for c in range(DC)])
        if lo == 0:
            pieces.append([(wd_v[:, i:i + FC // 2, :], (i * D, FC // 2 * D, FC // 2),
                            [w[:, i:i + FC // 2, :] for w in wd_s]) for i in (0, FC // 2)])
    pieces.append([(wk_v, (0, DC * KV * E, DC), [w[:, :, :] for w in wk_s]),
                   (wv_v, (DC * KV * E, DC * KV * E, DC), [w[:, :, :] for w in wv_s])])
    for c in range(DC):
        pieces.append([(wq_v[:, c:c + 1, :], (0, H * E, 1), [w[:, c:c + 1, :] for w in wq_s])])
    for i in range(2):
        hs = slice(i * H // 2, (i + 1) * H // 2)
        pieces.append([(wo_v[:, hs, :], (0, H // 2 * D, H // 2), [w[:, hs, :] for w in wo_s])])
    FFN_PIECES = 3
    DVE_PARTS = (0, 4, 5)
    POOL_PARTS = (1, 2, 3)
    FFN_PARTS = sum(len(p) for p in pieces[:FFN_PIECES])
    ALL_PARTS = sum(len(p) for p in pieces)

    POOL_TILES = (3, 2)
    DVE_TILES = (1, 0)

    def raw_view(k, at):
        start, width, n = at
        return raw[k % RAW_SLOTS][:, start:start + width].rearrange("p (a n) -> p a n", a=n)

    def parts():
        n = 0
        for k, piece in enumerate(pieces):
            for _, at, dst in piece:
                yield n, k, at, dst
                n += 1

    def landed(eng, k):
        loaded, start = (raw_in, 0) if k < FFN_PIECES else (attn_in, FFN_PIECES)
        eng.wait_ge(loaded[k % RAW_SLOTS], 16 * sum(
            len(pieces[i]) for i in range(start, k + 1) if i % RAW_SLOTS == k % RAW_SLOTS))

    banks, banks_last = ring(), ring(last=True)

    block = ctx.enter_context(nc.Block())

    @block.sync
    def _(sp):
        def load_piece(k):
            for src, at, _ in pieces[k]:
                sp.dma_start(raw_view(k, at), src).then_inc(raw_in[k % RAW_SLOTS], 16)

        def load_tokens(b):
            sp.dma_start(x_row[b][:], x_v[b]).then_inc(x_in[b], 16)

        load_tokens(0)
        load_tokens(1)
        sp.dma_start(ident[:], ident_in).then_inc(ident_loaded, 16)
        load_piece(0)
        load_tokens(2)
        load_tokens(3)
        load_piece(1)
        sp.dma_start(mask[:], mask_in).then_inc(const_in, 16)
        sp.dma_start(bias[:], bqkv).then_inc(const_in, 16)
        sp.dma_start(rowc[:], rows).then_inc(const_in, 16)
        sp.wait_ge(ffn_split_dve, 1)
        sp.wait_ge(ffn_split_pool, 1)
        load_piece(2)
        sp.sem_inc(g_free, 1)
        for b in range(B):
            sp.wait_ge(g_made, b + 1)
            sp.dma_start(g_v[b], g_out[:]).then_inc(g_stored, 16)
            sp.wait_ge(g_stored, 16 * b + 16)
            sp.sem_inc(g_free, 1)
        sp.wait_ge(down_done, B)
        for b in range(B):
            sp.dma_start(x_b[:], x_v[b]).then_inc(x_b_in, 16)
            sp.dma_start(g_b[:], g_v[b]).then_inc(g_b_in, 16)
            if b < B - 1:
                sp.wait_ge(out_made, 2 * b + 2)
                sp.dma_start(out_v[b], res[:]).then_inc(out_stored, 16)
                sp.wait_ge(out_stored, 16 * b + 16)
        for t in (3, 1, 2, 0):
            if t in POOL_TILES:
                sp.wait_ge(tile_out_pool, POOL_TILES.index(t) + 1)
            else:
                sp.wait_ge(tile_out_dve, DVE_TILES.index(t) + 1)
            sp.dma_start(out_v[B - 1][:, t, :], res[:, t, :]).then_inc(out_stored, 16)
        sp.wait_ge(out_stored, 16 * (B - 1 + T))

    @block.gpsimd
    def _(pool):
        nc.gpsimd.memset(neghalf[:], -0.5).then_inc(pool_chain, 1)
        pool.wait_ge(pool_chain, 1)

        def root1(b):
            pool.wait_ge(var_made, b + 1)
            nc.gpsimd.tensor_tensor(norm[:, b * T:(b + 1) * T, 1], ve1[:, b * T:(b + 1) * T], neghalf[:],
                                    ALU.pow).then_inc(rstd_made, 1)

        def ffn_low(part):
            for n, k, at, (hi, lo) in parts():
                if n == part:
                    pool.wait_ge(ffn_hi, n + 1)
                    nc.gpsimd.tensor_tensor(lo, raw_view(k, at), f32(hi), ALU.subtract).then_inc(ffn_split_pool, 1)

        root1(0)
        root1(1)
        ffn_low(POOL_PARTS[0])
        root1(2)
        root1(3)
        for part in POOL_PARTS[1:]:
            ffn_low(part)

        def load_piece(k):
            for src, at, _ in pieces[k]:
                pool.dma_start(raw_view(k, at), src).then_inc(attn_in[k % RAW_SLOTS], 16)

        pool.wait_ge(ffn_split_pool, len(POOL_PARTS))
        load_piece(FFN_PIECES)
        pool.wait_ge(ffn_split_dve, len(DVE_PARTS))
        load_piece(FFN_PIECES + 1)
        done_parts = FFN_PARTS
        for n, k, at, (hi, lo) in parts():
            if k >= FFN_PIECES:
                landed(pool, k)
                nc.gpsimd.tensor_copy(hi, raw_view(k, at)).then_inc(attn_hi, 1)
                pool.wait_ge(attn_hi, n - FFN_PARTS + 1)
                nc.gpsimd.tensor_tensor(lo, raw_view(k, at), f32(hi), ALU.subtract).then_inc(attn_split, 1)
                if n + 1 == done_parts + len(pieces[k]):
                    done_parts = n + 1
                    if k + RAW_SLOTS < len(pieces):
                        pool.wait_ge(attn_split, done_parts - FFN_PARTS)
                        load_piece(k + RAW_SLOTS)

        def over_tiles(row):
            return row.rearrange("p (a n) -> p a n", a=1).to_broadcast([P, T // 2, D])

        def residual(b):
            pool.wait_ge(gelu_done, b + 1)
            pool.wait_ge(xn_b_made, b + 1)
            nc.gpsimd.tensor_tensor(res[:], res[:], xn_b[:], ALU.add).then_inc(res_made, 1)

        def root(b):
            pool.wait_ge(var3_made, b + 1)
            nc.gpsimd.tensor_tensor(rstd3[:], ve3[:], neghalf[:], ALU.pow).then_inc(rstd3_made, 1)

        def out_piece(i):
            op, half = divmod(i, 2)
            tiles = slice(half * T // 2, (half + 1) * T // 2)
            other, how = ((over_tiles(gamma_row), ALU.mult), (over_tiles(beta_row), ALU.add),
                          (g_b[:, tiles], ALU.mult), (x_b[:, tiles], ALU.add))[op]

            def work(b):
                if i == 0:
                    pool.wait_ge(z_made, b + 1)
                    pool.wait_ge(g_b_in, 16 * b + 16)
                if op:
                    pool.wait_ge(pool_chain, b * 6 + i)
                ins = nc.gpsimd.tensor_tensor(res[:, tiles], res[:, tiles], other, how)
                ins.then_inc(pool_chain if op < 3 else out_made, 1)
            return work

        works = {"residual": residual, "root": root, **{f"out{i}": out_piece(i) for i in range(8)}}

        def steps(b, order, ends=()):
            for step in order:
                if step[0] == "s":
                    _, u, g = step
                    pool.wait_ge(inv_made, b * SCORES_ALL + u * G + g + 1)
                    p = probs[tile_of(u)][:, g, :]
                    nc.gpsimd.tensor_tensor(p, p, inv[:, u % UNITS, g:g + 1].to_broadcast([P, (tile_of(u) + 1) * P]),
                                            ALU.mult).then_inc(probs_made, 1)
                behind_word(ends, works, b, step)

        steps(0, segment(-1, text=AHEAD))
        steps(0, segment(0))
        with pool.Fori(0, B - 1) as b:
            for kv in range(1, KV):
                steps(b, segment(kv))
            steps(b, segment(KV), ROW_END_POOL)
        for kv in range(1, KV):
            steps(B - 1, segment(kv, last=kv == KV - 1))

        def tile_root_of(t):
            pool.wait_ge(tile_var, T - t)
            nc.gpsimd.tensor_tensor(rstd3[:, t:t + 1], ve3[:, t:t + 1], neghalf[:, 0:1], ALU.pow).then_inc(tile_root, 1)

        def tile_end(t):
            n = POOL_TILES.index(t)
            pool.wait_ge(tile_normed, n + 1)
            pool.wait_ge(g_b_in, 16 * B)
            r = res[:, t, :]
            for i, (other, op) in enumerate(((gamma_row, ALU.mult), (beta_row, ALU.add), (g_b[:, t, :], ALU.mult))):
                nc.gpsimd.tensor_tensor(r, r, other, op).then_inc(tile_chain_pool, 1)
                pool.wait_ge(tile_chain_pool, 3 * n + i + 1)
            nc.gpsimd.tensor_tensor(r, r, x_b[:, t, :], ALU.add).then_inc(tile_out_pool, 1)

        tile_root_of(3)
        tile_end(3)
        tile_root_of(2)
        tile_root_of(1)
        tile_root_of(0)
        tile_end(2)

    @block.scalar
    def _(act):
        def ffn_high(*which):
            for n, k, at, (hi, lo) in parts():
                if n in which:
                    landed(act, k)
                    nc.scalar.activation(hi, raw_view(k, at), ACT.Copy).then_inc(ffn_hi, 1)

        def xT_high(b):
            for c in range(DC):
                act.wait_ge(xT_done, b * DC + c + 1)
                nc.scalar.activation(xnT[0][:, c, b * L:(b + 1) * L], xT_ps[b][c], ACT.Copy).then_inc(xT_hi, 1)

        def gate_part(b, c):
            act.wait_ge(gate_done, b * FC + c + 1)
            nc.scalar.activation(gate[:, c % 2], gate_ps[c % 2], ACT.Silu).then_inc(gate_silu, 1)

        def hid_high(b, c):
            act.wait_ge(hid_made, b * FC + c + 1)
            nc.scalar.activation(hidT[c % 2][0][:], hid[:, c % 2], ACT.Copy).then_inc(hid_hi, 1)

        def silu_out(b):
            act.wait_ge(g_free, b + 1)
            act.wait_ge(down_done, b + 1)
            nc.scalar.activation(g_out[:], down_ps[:, :, 0:D], ACT.Silu).then_inc(g_made, 1)

        act.wait_ge(table_warm, 1)
        nc.scalar.activation(warm[:], warm[:], ACT.Silu).then_inc(table_warm, 1)
        ffn_high(0, 1)
        xT_high(0)
        xT_high(1)
        gate_part(0, 0)
        ffn_high(2, 3)
        xT_high(2)
        xT_high(3)
        hid_high(0, 0)
        for c in range(1, FC):
            gate_part(0, c)
            hid_high(0, c)
            if c == 1:
                ffn_high(4, 5)

        with act.Fori(1, B) as b:
            gate_part(b, 0)
            silu_out(b - 1)
            for c in range(FC):
                if c:
                    gate_part(b, c)
                hid_high(b, c)

        def gelu(b):
            act.wait_ge(x_b_in, 16 * b + 16)
            act.wait_ge(y_added, b * UNITS + UNITS)
            nc.scalar.activation(res[:], y[:], ACT.Gelu).then_inc(gelu_done, 1)

        def tile_gelu_of(u):
            act.wait_ge(x_b_in, 16 * B)
            act.wait_ge(y_added, (B - 1) * UNITS + u + 1)
            t = tile_of(u)
            nc.scalar.activation(res[:, t, :], y[:, t, :], ACT.Gelu).then_inc(tile_gelu, 1)

        def steps(b, order, ends=(), end=False):
            for step in scalar_steps(order):
                if step[0] in "kwq":
                    ps = ring_ps[banks[step][0]]
                    n = proj_index(step)
                    kv = step[1] % KV
                    act.wait_ge(proj_done, b * PROJ_ALL + n + 1)
                    if step[0] == "k":
                        nc.scalar.activation(k_first[:], ps[:, 0:P], ACT.Identity,
                                             bias=bias[:, H + kv:H + kv + 1])
                        nc.scalar.activation(kT[0][:], ps, ACT.Identity,
                                             bias=bias[:, H + kv:H + kv + 1]).then_inc(proj_hi, 1)
                    elif step[0] == "q":
                        h = step[2] * KV + kv
                        nc.scalar.activation(q_first[:, step[2], :], ps[:, 0:P], ACT.Identity,
                                             bias=bias[:, h:h + 1])
                        nc.scalar.activation(qT[step[2]][0][:], ps, ACT.Identity,
                                             bias=bias[:, h:h + 1]).then_inc(proj_hi, 1)
                    else:
                        nc.scalar.activation(v_s[kv % 2][0][:].rearrange("p t e -> p (t e)"), ps,
                                             ACT.Copy).then_inc(proj_hi, 1)
                elif step[0] == "s":
                    _, u, g = step
                    p = probs[tile_of(u)][:, g, :]
                    act.wait_ge(masked, b * SCORES_ALL + u * G + g + 1)
                    nc.scalar.activation(p, p, ACT.Exp, bias=least[:, u % UNITS, g:g + 1], scale=-1.0,
                                         accum_out=total[:, u % UNITS, g:g + 1]).then_inc(exp_done, 1)
                elif step[0] == "t":
                    r = pair_index(*step[1:])
                    act.wait_ge(probsT_done, b * PAIRS + r + 1)
                    ps, (hi, _) = transposed(step, end)
                    nc.scalar.activation(hi[:], ps, ACT.Copy).then_inc(probsT_hi, 1)
                elif step[0] == "p" and step[2] == tile_of(step[1]):
                    act.wait_ge(ctx_done, b * UNITS + step[1] + 1)
                    nc.scalar.activation(cT[0][:], ctx_ps, ACT.Copy).then_inc(ctx_hi, 1)
                behind_word(ends, {"gelu": gelu}, b, step)
                if end:
                    works_behind(LAST_ACT, {"gelu": tile_gelu_of}, step)

        steps(0, segment(-1, text=FIRST))
        silu_out(B - 1)
        steps(0, segment(-1, text=AHEAD))
        steps(0, segment(0))
        with act.Fori(0, B - 1) as b:
            for kv in range(1, KV):
                steps(b, segment(kv))
            steps(b, segment(KV), ROW_END_ACT)
        for kv in range(1, KV - 1):
            steps(B - 1, segment(kv))
        steps(B - 1, segment(KV - 1, last=True), end=True)
        tile_gelu_of(LAST + 3)

    @block.vector
    def _(dve):
        nc.vector.memset(warm[:], 0.0).then_inc(table_warm, 1)

        def mean_and_variance(b):
            dve.wait_ge(x_in[b], 16)
            for t in range(T):
                last = nc.vector.bn_stats(stats1[:, b * T + t, :], x_row[b][:, t, :])
            last.then_inc(stats_done, 1)
            dve.wait_ge(stats_done, b + 1)
            for t in range(b * T, (b + 1) * T):
                last = nc.vector.bn_aggr(norm[:, t, :], stats1[:, t, :])
            last.then_inc(aggr_done, 1)
            dve.wait_ge(aggr_done, b + 1)
            nc.vector.tensor_scalar(ve1[:, b * T:(b + 1) * T], norm[:, b * T:(b + 1) * T, 1], EPS, None,
                                    ALU.add).then_inc(var_made, 1)

        def normalise(b):
            dve.wait_ge(rstd_made, b + 1)
            if b >= 2:
                dve.wait_ge(xT_done, (b - 1) * DC)
            for t in range(T):
                last = nc.vector.tensor_scalar(xn[:, b % 2, t, :], x_row[b][:, t, :], norm[:, b * T + t, 0:1],
                                               norm[:, b * T + t, 1:2], ALU.subtract, ALU.mult)
            last.then_inc(xn_made, 1)

        def xT_low(b):
            for c in range(DC):
                dve.wait_ge(xT_hi, b * DC + c + 1)
                part = [w[:, c, b * L:(b + 1) * L] for w in xnT]
                nc.vector.tensor_tensor(part[1], xT_ps[b][c], f32(part[0]), ALU.subtract).then_inc(xT_split, 1)

        def ffn_low(*which):
            for n, k, at, (hi, lo) in parts():
                if n in which:
                    dve.wait_ge(ffn_hi, n + 1)
                    nc.vector.tensor_tensor(lo, raw_view(k, at), f32(hi), ALU.subtract).then_inc(ffn_split_dve, 1)

        def hid_part(b, c):
            dve.wait_ge(up_done, b * FC + c + 1)
            dve.wait_ge(gate_silu, b * FC + c + 1)
            nc.vector.tensor_tensor(hid[:, c % 2], gate[:, c % 2], up_ps[c % 2], ALU.mult).then_inc(hid_made, 1)

        def hid_low(b, c):
            dve.wait_ge(hid_hi, b * FC + c + 1)
            nc.vector.tensor_tensor(hidT[c % 2][1][:], hid[:, c % 2], f32(hidT[c % 2][0][:]),
                                    ALU.subtract).then_inc(hid_split, 1)

        mean_and_variance(0)
        mean_and_variance(1)
        normalise(0)
        normalise(1)
        xT_low(0)
        ffn_low(DVE_PARTS[0])
        xT_low(1)
        mean_and_variance(2)
        mean_and_variance(3)
        normalise(2)
        normalise(3)
        hid_part(0, 0)
        xT_low(2)
        xT_low(3)
        hid_low(0, 0)
        for c in range(1, FC):
            hid_part(0, c)
            hid_low(0, c)
            if c == 1:
                ffn_low(*DVE_PARTS[1:])

        with dve.Fori(1, B) as b:
            for c in range(FC):
                hid_part(b, c)
                hid_low(b, c)

        def low_part(step, b, end):
            if step[0] == "t":
                r = pair_index(*step[1:])
                dve.wait_ge(probsT_hi, b * PAIRS + r + 1)
                ps, (hi, lo) = transposed(step, end)
                nc.vector.tensor_tensor(lo[:], ps, f32(hi[:]), ALU.subtract).then_inc(probsT_split, 1)
            elif step[0] in "kwq":
                ps = ring_ps[banks[step][0]]
                kv = step[1] % KV
                dve.wait_ge(proj_hi, b * (PROJ_ALL - KV) + highs_done(step))
                if step[0] == "w":
                    hi, lo = (w[:].rearrange("p t e -> p (t e)") for w in v_s[kv % 2])
                    nc.vector.tensor_tensor(lo, ps, f32(hi), ALU.subtract).then_inc(proj_split, 1)
                else:
                    h = H + kv if step[0] == "k" else step[2] * KV + kv
                    hi, lo = kT if step[0] == "k" else qT[step[2]]
                    nc.vector.scalar_tensor_tensor(lo[:], ps, bias[:, h:h + 1], f32(hi[:]),
                                                   ALU.add, ALU.subtract).then_inc(proj_split, 1)
            else:
                dve.wait_ge(ctx_hi, b * UNITS + step[1] + 1)
                hi, lo = cT
                nc.vector.tensor_tensor(lo[:], ctx_ps, f32(hi[:]), ALU.subtract).then_inc(ctx_split, 1)

        def xn_again(b):
            dve.wait_ge(x_b_in, 16 * b + 16)
            for t in range(T):
                at = norm[:, bass.ds(b * T + t, 1), :]
                last = nc.vector.tensor_scalar(xn_b[:, t, :], x_b[:, t, :], at[:, 0, 0:1], at[:, 0, 1:2],
                                               ALU.subtract, ALU.mult)
            last.then_inc(xn_b_made, 1)

        def statistics(b):
            dve.wait_ge(res_made, b + 1)
            for t in range(T):
                last = nc.vector.bn_stats(stats3[:, t, :], res[:, t, :])
            last.then_inc(stats3_done, 1)
            dve.wait_ge(stats3_done, b + 1)
            nc.vector.memset(ve3[:], EPS)
            for t in range(T):
                last = nc.vector.bn_aggr(mv3[:, t, :], stats3[:, t, :])
            last.then_inc(aggr3_done, 1)
            dve.wait_ge(aggr3_done, b + 1)
            nc.vector.tensor_tensor(ve3[:], mv3[:, :, 1], ve3[:], ALU.add).then_inc(var3_made, 1)

        def norm_again(b):
            dve.wait_ge(rstd3_made, b + 1)
            for t in range(T):
                last = nc.vector.tensor_scalar(res[:, t, :], res[:, t, :], mv3[:, t, 0:1], rstd3[:, t:t + 1],
                                               ALU.subtract, ALU.mult)
            last.then_inc(z_made, 1)

        def tile_statistics(u):
            i, t = u - LAST, tile_of(u)
            dve.wait_ge(tile_gelu, i + 1)
            nc.vector.tensor_tensor(res[:, t, :], res[:, t, :], xn_b[:, t, :], ALU.add).then_inc(tile_chain_dve, 1)
            dve.wait_ge(tile_chain_dve, i * 3 + 1)
            nc.vector.bn_stats(stats3[:, t, :], res[:, t, :]).then_inc(tile_chain_dve, 1)
            dve.wait_ge(tile_chain_dve, i * 3 + 2)
            nc.vector.bn_aggr(mv3[:, t, :], stats3[:, t, :]).then_inc(tile_chain_dve, 1)
            dve.wait_ge(tile_chain_dve, i * 3 + 3)
            nc.vector.tensor_scalar(ve3[:, t:t + 1], mv3[:, t, 1:2], EPS, None, ALU.add).then_inc(tile_var, 1)

        def tile_output(u):
            i, t = u - LAST, tile_of(u)
            r = res[:, t, :]
            dve.wait_ge(tile_root, i + 1)
            if t in POOL_TILES:
                nc.vector.tensor_scalar(r, r, mv3[:, t, 0:1], rstd3[:, t:t + 1],
                                        ALU.subtract, ALU.mult).then_inc(tile_normed, 1)
                return
            done = 3 * DVE_TILES.index(t)
            dve.wait_ge(g_b_in, 16 * B)
            nc.vector.scalar_tensor_tensor(r, r, mv3[:, t, 0:1], gamma_row, ALU.subtract, ALU.mult).then_inc(tile_scaled, 1)
            dve.wait_ge(tile_scaled, done + 1)
            nc.vector.scalar_tensor_tensor(r, r, rstd3[:, t:t + 1], beta_row, ALU.mult, ALU.add).then_inc(tile_scaled, 1)
            dve.wait_ge(tile_scaled, done + 2)
            nc.vector.tensor_tensor(r, r, g_b[:, t, :], ALU.mult).then_inc(tile_scaled, 1)
            dve.wait_ge(tile_scaled, done + 3)
            nc.vector.tensor_tensor(r, r, x_b[:, t, :], ALU.add).then_inc(tile_out_dve, 1)

        def steps(b, order, ends=(), row_ends=(), end=False):
            of = banks_last if end else banks
            for step in vector_steps(order):
                if step[0] == "masked":
                    _, u, g = step
                    t = tile_of(u)
                    n = u * G + g
                    ps = ring_ps[of["s", u, g][0]]
                    dve.wait_ge(scores_done, b * SCORES_ALL + n + 1)
                    nc.vector.memset(total[:, u % UNITS, g:g + 1], 0.0)
                    nc.vector.tensor_tensor_reduce(
                        out=probs[t][:, g, :], in0=ps[:, 0:(t + 1) * P],
                        in1=mask[:, (T - 1 - t) * P:], scale=-SCALE, scalar=BIG, op0=ALU.add, op1=ALU.min,
                        accum_out=least[:, u % UNITS, g:g + 1]).then_inc(masked, 1)
                elif step[0] == "inv":
                    _, u, g = step
                    dve.wait_ge(exp_done, b * SCORES_ALL + u * G + g + 1)
                    nc.vector.reciprocal(inv[:, u % UNITS, g:g + 1], total[:, u % UNITS, g:g + 1]).then_inc(inv_made, 1)
                elif step[0] == "low":
                    low_part(step[1], b, end)
                elif step[0] == "v":
                    n = proj_index(step)
                    ps = ring_ps[of[step][0]]
                    dve.wait_ge(proj_done, b * PROJ_ALL + n + 1)
                    h = H + KV + step[1] % KV
                    nc.vector.tensor_scalar(vT[:], ps, bias[:, h:h + 1], None,
                                            ALU.add).then_inc(proj_split, 1)
                else:
                    u = step[1]
                    t = tile_of(u)
                    dve.wait_ge(y_done, b * UNITS + u + 1)
                    base = bo_row if kv_of(u) % KV == 0 else y[:, t, :]
                    nc.vector.tensor_tensor(y[:, t, :], y_ps, base, ALU.add).then_inc(y_added, 1)
                for at, work in ends:
                    if step == at:
                        work(b)
                if end:
                    works_behind(LAST_DVE, {"statistics": tile_statistics, "output": tile_output},
                                 step[1] if step[0] == "low" else step)
                behind_word(row_ends, {"statistics": statistics, "norm": norm_again}, b,
                            step[1] if step[0] == "low" else ("s", *step[1:]) if step[0] == "masked" else None)

        def low_of(kv, *step):
            return "low", (step[0], kv, *step[1:])

        steps(0, segment(-1, text=FIRST))
        steps(0, segment(-1, text=AHEAD))
        steps(0, segment(0))
        with dve.Fori(0, B - 1) as b:
            for kv in range(1, KV):
                steps(b, segment(kv), ((low_of(kv + 1, "k"), xn_again),) if kv == KV - 1 else ())
            steps(b, segment(KV), row_ends=ROW_END_DVE)
        for kv in range(1, KV - 1):
            steps(B - 1, segment(kv))
        steps(B - 1, segment(KV - 1, last=True), ((("masked", LAST + T - 1, 0), xn_again),), end=True)
        tile_output(LAST + 1)
        tile_statistics(LAST + 3)
        tile_output(LAST + 2)
        tile_output(LAST + 3)

    @block.tensor
    def _(pe):
        def product(dst, left, right, first, last):
            for i, (a, c) in enumerate(PASSES):
                ins = nc.tensor.matmul(dst, left[a], right[c], start=first and i == 0,
                                       stop=last and i == len(PASSES) - 1)
            return ins

        def transpose_tokens(b):
            pe.wait_ge(xn_made, b + 1)
            for c in range(DC):
                for t in range(T):
                    last = nc.tensor.transpose(xT_ps[b][c][:, t * P:(t + 1) * P],
                                               xn[:, b % 2, t, c * P:(c + 1) * P], ident[:])
                last.then_inc(xT_done, 1)

        def gate_up(b, c, first=False):
            if c >= 2:
                pe.wait_ge(hid_made, b * FC + c - 1)
            if first and c in (0, FC // 2):
                pe.wait_ge(ffn_split_dve, 1 if c == 0 else len(DVE_PARTS))
                pe.wait_ge(ffn_split_pool, 1)
            for i, (ps, done) in enumerate(((gate_ps, gate_done), (up_ps, up_done))):
                at = i * F + c * P
                for k in range(DC):
                    last = product(ps[c % 2], [w[:, k, at:at + P] for w in wgu_s],
                                   [w[:, k, bass.ds(b * L, L)] for w in xnT], k == 0, k == DC - 1)
                last.then_inc(done, 1)

        def down(b, c, first=False):
            if first and c in (0, FC // 2):
                pe.wait_ge(ffn_split_pool, 2 if c == 0 else len(POOL_PARTS))
            pe.wait_ge(hid_split, b * FC + c + 1)
            for t in range(T):
                last = product(down_ps[:, t, 0:D], [w[:, t * P:(t + 1) * P] for w in hidT[c % 2]],
                               [w[:, c, :] for w in wd_s], c == 0, c == FC - 1)
            return last

        def ring_bank(b, step, of=banks):
            bank, before = of[step]
            if before and before[0] == "s":
                pe.wait_ge(masked, b * SCORES_ALL + before[1] * G + before[2] + 1)
            elif before:
                pe.wait_ge(proj_split, b * PROJ_ALL + proj_index(before) + 1)
            return ring_ps[bank]

        def project(b, step):
            kind, kv = step[0], step[1]
            ps = ring_bank(b, step)
            if kind == "w":
                pe.wait_ge(proj_split, b * PROJ_ALL + proj_index(("v", kv)) + 1)
                for j in range(T):
                    last = nc.tensor.transpose(ps[:, j * P:(j + 1) * P], vT[:, j * P:(j + 1) * P], ident[:])
            else:
                w_s = {"k": wk_s, "v": wv_s, "q": wq_s}[kind]
                at = (step[2] * KV + kv % KV if kind == "q" else kv % KV) * E
                row = b + kv // KV
                for c in range(DC):
                    last = product(ps, [w[:, c, at:at + E] for w in w_s],
                                   [w[:, c, bass.ds(row * L, L)] for w in xnT], c == 0, c == DC - 1)
            last.then_inc(proj_done, 1)

        def scores(b, u, g, of):
            t = tile_of(u)
            pe.wait_ge(proj_split, b * PROJ_ALL + max(map(proj_index, (("k", kv_of(u)), ("q", kv_of(u), g)))) + 1)
            ps = ring_bank(b, ("s", u, g), of)
            width = (t + 1) * P
            if t:
                last = product(ps[:, 0:width], [w[:, t * P:(t + 1) * P] for w in qT[g]],
                               [w[:, 0:width] for w in kT], True, True)
            else:
                last = nc.tensor.matmul(ps[:, 0:P], q_first[:, g, :], k_first[:], start=True, stop=True)
            last.then_inc(scores_done, 1)

        def transposes(b, u, j, end):
            r = pair_index(u, j)
            if j == 0:
                pe.wait_ge(probs_made, b * SCORES_ALL + (u + 1) * G)
            if pair_place(("t", u, j), end)[0]:
                pe.wait_ge(masked, B * SCORES_ALL)
            elif r >= 2:
                pe.wait_ge(probsT_split, b * PAIRS + r - 1)
            ps = transposed(("t", u, j), end)[0]
            for g in range(G):
                last = nc.tensor.transpose(ps[:, g * P:(g + 1) * P],
                                           probs[tile_of(u)][:, g, j * P:(j + 1) * P], ident[:])
            last.then_inc(probsT_done, 1)

        def values(b, u, j, end):
            r = pair_index(u, j)
            pe.wait_ge(probsT_split, b * PAIRS + r + 1)
            if j == 0:
                pe.wait_ge(proj_split, b * PROJ_ALL + proj_index(("w", kv_of(u))) + 1)
                if u:
                    pe.wait_ge(ctx_split, b * UNITS + u)
            last = product(ctx_ps, [w[:, j, :] for w in v_s[kv_of(u) % 2]], [w[:] for w in transposed(("t", u, j), end)[1]],
                           j == 0, j == tile_of(u))
            if j == tile_of(u):
                last.then_inc(ctx_done, 1)

        def output(b, u):
            pe.wait_ge(ctx_split, b * UNITS + u + 1)
            if u:
                pe.wait_ge(y_added, b * UNITS + u)
            for g in range(G):
                last = product(y_ps, [w[:, g * P:(g + 1) * P] for w in cT], [w[:, g * KV + kv_of(u) % KV, :] for w in wo_s],
                               g == 0, g == G - 1)
            last.then_inc(y_done, 1)

        def steps(b, order, end=False):
            of = banks_last if end else banks
            for step in order:
                if step[0] in "kvwq":
                    project(b, step)
                elif step[0] == "s":
                    scores(b, *step[1:], of)
                elif step[0] == "t":
                    transposes(b, *step[1:], end)
                elif step[0] == "p":
                    values(b, *step[1:], end)
                else:
                    output(b, step[1])

        def ffn_row(b, first=False, last=False):
            for c in range(1, FC):
                gate_up(b, c, first)
                if first and c == 1:
                    transpose_tokens(2)
                    transpose_tokens(3)
                    pe.wait_ge(xT_split, B * DC)
                down(b, c - 1, first)
            if last:
                pe.wait_ge(hid_made, B * FC)
                pe.wait_ge(attn_split, ALL_PARTS - FFN_PARTS)
                pe.wait_ge(const_in, 48)
                steps(0, segment(-1, text=FIRST))
            else:
                gate_next(b + 1)
            down(b, FC - 1).then_inc(down_done, 1)

        def gate_next(b):
            pe.wait_ge(hid_made, b * FC - 1)
            gate_up(b, 0)

        pe.wait_ge(ident_loaded, 16)
        transpose_tokens(0)
        transpose_tokens(1)
        pe.wait_ge(xT_split, 2 * DC)
        gate_up(0, 0, first=True)
        ffn_row(0, first=True)
        with pe.Fori(1, B - 1) as b:
            ffn_row(b)
        ffn_row(B - 1, last=True)

        steps(0, segment(-1, text=AHEAD))
        pe.wait_ge(g_made, B)
        steps(0, segment(0))
        with pe.Fori(0, B - 1) as b:
            for kv in range(1, KV):
                steps(b, segment(kv))
            steps(b, segment(KV))
        for kv in range(1, KV):
            steps(B - 1, segment(kv, last=kv == KV - 1), end=kv == KV - 1)

    ctx.close()




def kernel(**inputs):
    import concourse.bacc as bacc
    from concourse.bass_utils import run_bass_kernel_spmd

    def get(name):
        return np.asarray(inputs["L0_" + name])

    def by_head(a):
        return a.reshape(-1, E).T

    keys = np.arange(P)
    mask = np.zeros((P, L), np.float32)
    mask[:, L - P:] = np.where(keys[None, :] > keys[:, None], np.float32(MASK), np.float32(0))
    arrays = {
        "x": get("attn_x"),
        "wq": get("attn_Wq"),
        "wk": get("attn_Wk"),
        "wv": get("attn_Wv"),
        "wo": get("attn_Wo"),
        "wgu": get("ffn_w_gate_up").T,
        "wd": get("ffn_w_down").T,
        "bqkv": np.concatenate([by_head(get("attn_bq")), by_head(get("attn_bk")), by_head(get("attn_bv"))], axis=1),
        "rows": np.broadcast_to(np.stack([get("attn_bo"), get("attn_gamma"), get("attn_beta")]), (P, 3, D)),
        "ident": np.eye(P, dtype=np.float32),
        "mask": mask,
    }
    arrays = {f"in_{k}": np.ascontiguousarray(v) for k, v in arrays.items()}
    nc = bacc.Bacc("TRN2", target_bir_lowering=False, num_devices=1)
    args = [nc.dram_tensor(k, a.shape, F32, kind="ExternalInput").ap() for k, a in arrays.items()]
    g_scratch = nc.dram_tensor("g_scratch", (B, L, D), F32, kind="Internal").ap()
    out = nc.dram_tensor("out", (B, L, D), F32, kind="ExternalOutput").ap()
    build(nc, *args, g_scratch, out)
    r = run_bass_kernel_spmd(nc, [arrays], core_ids=[0])
    return r.results[0]["out"]
```
